# Optimizing a Trainium2 kernel written in Bass

```python
import numpy as np
import jax
import jax.numpy as jnp

def _softmax(x, axis=-1):
    return jax.nn.softmax(x, axis=axis)

def _gelu(x):
    return jax.nn.gelu(x, approximate=True)

def _silu(x):
    return jax.nn.silu(x)

def _sigmoid(x):
    return jax.nn.sigmoid(x)

def _layernorm(x, axis=-1, eps=1e-05):
    m = jnp.mean(x, axis=axis, keepdims=True)
    v = jnp.var(x, axis=axis, keepdims=True)
    return (x - m) / jnp.sqrt(v + eps)

def _scatter_add(tgt, idx, src, axis=0):
    return tgt.at[idx].add(src)

def _segment_sum(src, seg, n):
    return jax.ops.segment_sum(src, seg, n)
kernel_name = 'mk_hybrid_d1_jaxref_r4_5007ac'

def setup_inputs(seed: int=0):
    np.random.seed(seed)
    _w = jnp.asarray

    def _L0_attn_a_setup():
        import jax, jax.numpy as jnp
        import numpy as np
        key = jax.random.key(seed)
        k1, k2 = jax.random.split(key, 2)
        B, T, C = (8, 512, 256)
        x = jax.random.normal(k1, (B, T, C), dtype=jnp.float32)
        W = jax.random.normal(k2, (C, C), dtype=jnp.float32) * (1.0 / np.sqrt(C))
        b = jnp.zeros((C,), dtype=jnp.float32)
        return {'x': x, 'W': W, 'b': b}
    _L0_attn_a_in = _L0_attn_a_setup()

    def _L0_attn_b_setup():
        import jax, jax.numpy as jnp
        import numpy as np
        B, S, HID = (2, 1024, 256)
        NH, HD, W = (16, 64, 128)
        ROPE_THETA = 10000.0

        def _apply_rope(x):
            s, d = (x.shape[2], x.shape[3])
            pos = jnp.arange(s, dtype=jnp.float32)
            inv_freq = 1.0 / ROPE_THETA ** (jnp.arange(0, d, 2, dtype=jnp.float32) / d)
            ang = pos[:, None] * inv_freq[None, :]
            cos = jnp.tile(jnp.cos(ang), (1, 2))[None, None]
            sin = jnp.tile(jnp.sin(ang), (1, 2))[None, None]
            x1, x2 = jnp.split(x, 2, axis=-1)
            rot = jnp.concatenate([-x2, x1], axis=-1)
            return x * cos + rot * sin
        key = jax.random.key(seed)
        ks = jax.random.split(key, 9)
        sc = 0.02
        return {'hidden_states': jax.random.normal(ks[0], (B, S, HID), dtype=jnp.float32), 'Wq': jax.random.normal(ks[1], (NH * HD, HID), dtype=jnp.float32) * sc, 'bq': jnp.zeros((NH * HD,), dtype=jnp.float32), 'Wk': jax.random.normal(ks[2], (NH * HD, HID), dtype=jnp.float32) * sc, 'bk': jnp.zeros((NH * HD,), dtype=jnp.float32), 'Wv': jax.random.normal(ks[3], (NH * HD, HID), dtype=jnp.float32) * sc, 'bv': jnp.zeros((NH * HD,), dtype=jnp.float32), 'Wo': jax.random.normal(ks[4], (HID, NH * HD), dtype=jnp.float32) * sc, 'bo': jnp.zeros((HID,), dtype=jnp.float32)}
    _L0_attn_b_in = _L0_attn_b_setup()

    def _L0_ffn_setup():
        import jax, jax.numpy as jnp
        import numpy as np
        DIM = 256

        def _reference_tuple_inner(x, W_r, W_k, W_v, mu_r, mu_k):
            B, T, C = x.shape
            x_prev = jnp.concatenate([jnp.zeros((B, 1, C), x.dtype), x[:, :-1, :]], axis=1)
            xr = mu_r * x + (1.0 - mu_r) * x_prev
            xk = mu_k * x + (1.0 - mu_k) * x_prev
            r = jax.nn.sigmoid(jnp.einsum('btc,dc->btd', xr, W_r))
            k = jnp.einsum('btc,dc->btd', xk, W_k)
            k_act = jnp.square(jax.nn.relu(k))
            out = r * jnp.einsum('btc,dc->btd', k_act, W_v)
            new_state = x[:, -1, :]
            return (out, new_state)
        key = jax.random.key(seed)
        ks = jax.random.split(key, 6)
        B, T, C = (8, 512, DIM)
        x = jax.random.normal(ks[0], (B, T, C), dtype=jnp.float32)
        s = 1.0 / np.sqrt(C)
        W_r = jax.random.uniform(ks[1], (C, C), jnp.float32, -s, s)
        W_k = jax.random.uniform(ks[2], (C, C), jnp.float32, -s, s)
        W_v = jax.random.uniform(ks[3], (C, C), jnp.float32, -s, s)
        mu_r = jax.random.uniform(ks[4], (C,), jnp.float32)
        mu_k = jax.random.uniform(ks[5], (C,), jnp.float32)
        return {'x': x, 'W_r': W_r, 'W_k': W_k, 'W_v': W_v, 'mu_r': mu_r, 'mu_k': mu_k}
    _L0_ffn_in = _L0_ffn_setup()
    _d = {'L0_attn_a_x': _L0_attn_a_in['x'], 'L0_attn_a_W': _L0_attn_a_in['W'], 'L0_attn_a_b': _L0_attn_a_in['b'], 'L0_attn_b_Wq': _L0_attn_b_in['Wq'], 'L0_attn_b_bq': _L0_attn_b_in['bq'], 'L0_attn_b_Wk': _L0_attn_b_in['Wk'], 'L0_attn_b_bk': _L0_attn_b_in['bk'], 'L0_attn_b_Wv': _L0_attn_b_in['Wv'], 'L0_attn_b_bv': _L0_attn_b_in['bv'], 'L0_attn_b_Wo': _L0_attn_b_in['Wo'], 'L0_attn_b_bo': _L0_attn_b_in['bo'], 'L0_ffn_W_r': _L0_ffn_in['W_r'], 'L0_ffn_W_k': _L0_ffn_in['W_k'], 'L0_ffn_W_v': _L0_ffn_in['W_v'], 'L0_ffn_mu_r': _L0_ffn_in['mu_r'], 'L0_ffn_mu_k': _L0_ffn_in['mu_k']}
    _x0 = _d['L0_attn_a_x']
    _d['L0_attn_a_x'] = jax.random.normal(jax.random.fold_in(jax.random.key(seed), 1), (4, 2048, 256), dtype=_x0.dtype)
    del _x0
    return _d

def reference(L0_attn_a_x, L0_attn_a_W, L0_attn_a_b, L0_attn_b_Wq, L0_attn_b_bq, L0_attn_b_Wk, L0_attn_b_bk, L0_attn_b_Wv, L0_attn_b_bv, L0_attn_b_Wo, L0_attn_b_bo, L0_ffn_W_r, L0_ffn_W_k, L0_ffn_W_v, L0_ffn_mu_r, L0_ffn_mu_k):

    def _L0_attn_a_ref(x, W, b):
        import jax, jax.numpy as jnp
        import numpy as np
        v = jnp.einsum('btc,dc->btd', x, W) + b
        B, T, C = x.shape
        y = jnp.broadcast_to(v[:, 1:2, :], (B, T, C))
        return y

    def _L0_attn_b_ref(hidden_states, Wq, bq, Wk, bk, Wv, bv, Wo, bo):
        import jax, jax.numpy as jnp
        import numpy as np
        B, S, HID = (2, 1024, 256)
        NH, HD, W = (16, 64, 128)
        ROPE_THETA = 10000.0

        def _apply_rope(x):
            s, d = (x.shape[2], x.shape[3])
            pos = jnp.arange(s, dtype=jnp.float32)
            inv_freq = 1.0 / ROPE_THETA ** (jnp.arange(0, d, 2, dtype=jnp.float32) / d)
            ang = pos[:, None] * inv_freq[None, :]
            cos = jnp.tile(jnp.cos(ang), (1, 2))[None, None]
            sin = jnp.tile(jnp.sin(ang), (1, 2))[None, None]
            x1, x2 = jnp.split(x, 2, axis=-1)
            rot = jnp.concatenate([-x2, x1], axis=-1)
            return x * cos + rot * sin
        b, s, _ = hidden_states.shape

        def proj(Wm, bm):
            y = hidden_states @ Wm.T + bm
            return y.reshape(b, s, NH, HD).transpose(0, 2, 1, 3)
        q = _apply_rope(proj(Wq, bq))
        k = _apply_rope(proj(Wk, bk))
        v = proj(Wv, bv)
        nb = s // W
        qb = q.reshape(b, NH, nb, W, HD)
        kb = k.reshape(b, NH, nb, W, HD)
        vb = v.reshape(b, NH, nb, W, HD)
        zpad = jnp.zeros_like(kb[:, :, :1])
        kcat = jnp.concatenate([jnp.concatenate([zpad, kb[:, :, :-1]], axis=2), kb], axis=3)
        vcat = jnp.concatenate([jnp.concatenate([zpad, vb[:, :, :-1]], axis=2), vb], axis=3)
        scale = 1.0 / jnp.sqrt(jnp.asarray(HD, dtype=q.dtype))
        scores = jnp.einsum('bhnqd,bhnkd->bhnqk', qb, kcat) * scale
        qi = jnp.arange(W)[:, None]
        kj = jnp.arange(2 * W)[None, :]
        band = (kj >= qi) & (kj <= qi + W)
        nidx = jnp.arange(nb)[:, None, None]
        valid = band[None] & ((nidx > 0) | (kj[None] >= W))
        scores = jnp.where(valid[None, None], scores, jnp.asarray(-1e+30, scores.dtype))
        attn = jax.nn.softmax(scores, axis=-1)
        ctx = jnp.einsum('bhnqk,bhnkd->bhnqd', attn, vcat)
        merged = ctx.reshape(b, NH, s, HD).transpose(0, 2, 1, 3).reshape(b, s, NH * HD)
        return merged @ Wo.T + bo

    def _L0_ffn_ref(x, W_r, W_k, W_v, mu_r, mu_k):
        import jax, jax.numpy as jnp
        import numpy as np
        DIM = 256

        def _reference_tuple_inner(x, W_r, W_k, W_v, mu_r, mu_k):
            B, T, C = x.shape
            x_prev = jnp.concatenate([jnp.zeros((B, 1, C), x.dtype), x[:, :-1, :]], axis=1)
            xr = mu_r * x + (1.0 - mu_r) * x_prev
            xk = mu_k * x + (1.0 - mu_k) * x_prev
            r = jax.nn.sigmoid(jnp.einsum('btc,dc->btd', xr, W_r))
            k = jnp.einsum('btc,dc->btd', xk, W_k)
            k_act = jnp.square(jax.nn.relu(k))
            out = r * jnp.einsum('btc,dc->btd', k_act, W_v)
            new_state = x[:, -1, :]
            return (out, new_state)
        return _reference_tuple_inner(x, W_r, W_k, W_v, mu_r, mu_k)[0]
    x = L0_attn_a_x
    x = x + _L0_attn_a_ref(_layernorm(x, axis=-1), L0_attn_a_W, L0_attn_a_b)
    x = x + _L0_ffn_ref(_layernorm(x, axis=-1), L0_ffn_W_r, L0_ffn_W_k, L0_ffn_W_v, L0_ffn_mu_r, L0_ffn_mu_k)
    x = x + _L0_attn_b_ref(_layernorm(x, axis=-1), L0_attn_b_Wq, L0_attn_b_bq, L0_attn_b_Wk, L0_attn_b_bk, L0_attn_b_Wv, L0_attn_b_bv, L0_attn_b_Wo, L0_attn_b_bo)
    x = x + _L0_ffn_ref(_layernorm(x, axis=-1), L0_ffn_W_r, L0_ffn_W_k, L0_ffn_W_v, L0_ffn_mu_r, L0_ffn_mu_k)
    return x

_drawn_inputs = setup_inputs


def setup_inputs(seed=0):
    import zlib

    import numpy as np

    out = dict(_drawn_inputs(seed))
    spreads = {'L0_attn_a_b': (0.0, 0.1),
     'L0_attn_b_bq': (0.0, 0.8),
     'L0_attn_b_bk': (0.0, 0.8),
     'L0_attn_b_bv': (0.0, 0.1),
     'L0_attn_b_bo': (0.0, 0.1)}
    factors = {'L0_attn_b_Wq': 8.0, 'L0_attn_b_Wk': 8.0, 'L0_ffn_mu_r': 5.47}
    for name, (base, spread) in spreads.items():
        noise = np.random.default_rng([zlib.crc32(name.encode()), seed]).standard_normal(out[name].shape)
        drawn = base * np.exp(spread * noise) if base else spread * noise
        out[name] = jnp.asarray(drawn.astype(out[name].dtype))
    for name, factor in factors.items():
        out[name] = (out[name] * factor).astype(out[name].dtype)
    return out
```

```python
from contextlib import ExitStack

import concourse.bass as bass
import numpy as np
from concourse import mybir

F32 = mybir.dt.float32
F32R = mybir.dt.float32r
F16 = mybir.dt.float16
ALU = mybir.AluOpType
ACT = mybir.ActivationFunctionType
AX = mybir.AxisListType

P = 128
BATCH, SEQ, C = 4, 2048, 256
NBLK = BATCH * SEQ // P
BPB = SEQ // P
CK = C // P
EPS = 1e-5

HEADS, HD = 16, 64
QKV = HEADS * HD
GROUP = 4
NG = HEADS // GROUP
SCALE = 1.0 / float(np.sqrt(HD))
MASKED = -1e30
V_TOP = 2.0**14


class Need:

    def __init__(self, eng):
        self.eng = eng

    def __call__(self, sem, count):
        if not isinstance(count, int) or count > 0:
            self.eng.wait_ge(sem, count)


def identity(nc, pool, tile, made, n=1):
    nc.gpsimd.memset(tile[:, :], 0.0).then_inc(made, 1)
    pool.wait_ge(made, n)
    nc.gpsimd.affine_select(out=tile[:, :], in_=tile[:, :], compare_op=ALU.not_equal, fill=1.0,
                            base=0, pattern=[[-1, P]], channel_multiplier=1).then_inc(made, 1)


def ffn_phase(nc, sems, name, x_in, x_out, wr_t, wk_t, wv_t, mu_r, mu_k, value=None):
    CB = 4
    N = CB * P
    CHUNKS = NBLK // CB
    CPB = CHUNKS // BATCH
    SLOTS = 4
    R, K = 0, 1
    HIGH, LOW = 0, 1
    TERMS = ((HIGH, HIGH), (LOW, HIGH), (HIGH, LOW))

    def sem(what):
        return sems.enter_context(nc.semaphore(f"{name}_{what}"))

    with ExitStack() as mem:
        def sb(what, shape, dt=F32):
            return mem.enter_context(nc.sbuf_tensor(f"{name}_{what}", shape, dt))

        def bank(what):
            return mem.enter_context(nc.psum_tensor(f"{name}_{what}", [P, 2, 512], F32))

        x_raw = sb("x_raw", [P, 2, CB, C])
        x = sb("x", [P, SLOTS, CB, C])
        x_new = sb("x_new", [P, 2, CB, C])
        xn = sb("xn", [P, CB, C])
        stats = sb("stats", [P, CB, 6])
        mv = sb("mv", [P, CB, 2])
        veps = sb("veps", [P, CB])
        rstd = sb("rstd", [P, CB])
        power = sb("power", [P, CB])
        one = sb("one", [P, CB])
        eps = sb("eps", [P, CB])
        carrier = sb("carrier", [P, 1])
        xt = sb("xt", [P, 2, CK, N + 1])
        zero = sb("zero", [P, CK, 1])
        step = sb("step", [P, CK, N])
        mix = sb("mix", [P, 2, CK, N])
        mix_h = sb("mix_h", [P, 2, CK, N], F32R)
        mix_l = sb("mix_l", [P, 2, CK, N], F32R)
        relu = sb("relu", [P, CK, N])
        act = sb("act", [P, CK, N])
        act_h = sb("act_h", [P, CK, N], F32R)
        act_l = sb("act_l", [P, CK, N], F32R)
        gate = sb("gate", [P, 2, 2 * C])
        gated = sb("gated", [P, 2, 2 * C])
        w_raw = sb("w_raw", [P, 3, CK, C])
        w_h = sb("w_h", [P, 3, CK, C], F32R)
        w_l = sb("w_l", [P, 3, CK, C], F32R)
        mu = sb("mu", [P, 2, CK])
        ident = sb("ident", [P, P])
        WR, WK, WV = range(3)

        t_ps = bank("t_ps")
        k_ps = bank("k_ps")
        r_ps = bank("r_ps")
        v_ps = bank("v_ps")

        load = [sem(f"load{s}") for s in range(2)]
        stored = [sem(f"stored{s}") for s in range(2)]
        consts = sem("consts")
        ident_made = sem("ident_made")
        w_high = sem("w_high")
        w_low = sem("w_low")
        valued = sem("valued")
        stats_made = sem("stats_made")
        mv_made = sem("mv_made")
        veps_made = sem("veps_made")
        rstd_made = sem("rstd_made")
        xn_made = sem("xn_made")
        t_done = sem("t_done")
        xt_made = sem("xt_made")
        step_made = sem("step_made")
        mix_made = sem("mix_made")
        mixh_made = sem("mixh_made")
        mixl_made = sem("mixl_made")
        k_done = sem("k_done")
        relu_made = sem("relu_made")
        act_made = sem("act_made")
        acth_made = sem("acth_made")
        actl_made = sem("actl_made")
        r_done = sem("r_done")
        gate_made = sem("gate_made")
        v_done = sem("v_done")
        gated_made = sem("gated_made")
        x_made = sem("x_made")

        if value is not None:
            value_wt, value_b = value
            wa = sb("wa", [P, CK, C])
            ba = sb("ba", [P, C])
            vb = sb("vb", [P, BATCH, C])
            value_in = sem("value_in")
            wa_in = sem("wa_in")
            va_stats = sem("va_stats")
            va_mv = sem("va_mv")
            va_rstd = sem("va_rstd")
            va_xn = sem("va_xn")
            va_t = sem("va_t")
            va_xt = sem("va_xt")
            va_done = sem("va_done")
            vb_made = sem("vb_made")
            value_now = sb("value_now", [P, C])
            value_now_made = sem("value_now_made")

        def chunk(ap, c):
            return ap[:, bass.ts(c, CB), :]

        block = mem.enter_context(nc.Block())

        def over_batches(body):
            def run(eng):
                body(eng, 0)
                with eng.Fori(1, BATCH - 1) as b:
                    body(eng, b)
                body(eng, BATCH - 1)
            return run

        def before(b, s):
            return not isinstance(b, int) or b * CPB + s > 0

        def remain(b, s, ahead):
            return not isinstance(b, int) or b * CPB + s + ahead < CHUNKS

        @block.sync
        def _(sp):
            need = Need(sp)
            if value is not None:
                for b in range(BATCH):
                    sp.dma_start(xn[:, b, :], x_in[1, b * BPB, :].partition_broadcast(P)).then_inc(value_in, 16)
            def fetch(c, s):
                sp.dma_start(x_raw[:, s % 2, :, :], chunk(x_in, c)).then_inc(load[s % 2], 16)

            for s in range(2):
                fetch(s, s)
            for s in range(2, 4):
                sp.wait_ge(valued, s - 1)
                fetch(s, s)

            def store(c, s):
                sp.dma_start(chunk(x_out, c), x_new[:, s % 2, :, :]).then_inc(stored[s % 2], 16)

            def batch(sp, b):
                for s in range(CPB):
                    c = b * CPB + s
                    if before(b, s):
                        sp.wait_ge(x_made, c)
                        store(c - 1, s + 1)
                    if remain(b, s, 4):
                        sp.wait_ge(valued, c + 3)
                        fetch(c + 4, s)
            over_batches(batch)(sp)
            sp.wait_ge(x_made, CHUNKS)
            store(CHUNKS - 1, 1)
            for s in range(2):
                sp.wait_ge(stored[s], 16 * CHUNKS // 2)

        @block.gpsimd
        def _(pool):
            need = Need(pool)
            nc.gpsimd.memset(power[:, :], -0.5).then_inc(ident_made, 1)
            nc.gpsimd.memset(eps[:, :], EPS)
            nc.gpsimd.memset(one[:, :], 1.0)
            nc.gpsimd.memset(zero[:, :, :], 0.0).then_inc(ident_made, 1)
            identity(nc, pool, ident, ident_made, 3)

            def inverse_std(n, made):
                nc.gpsimd.tensor_tensor(veps[:, :], mv[:, :, 1], eps[:, :], ALU.add).then_inc(veps_made, 1)
                pool.wait_ge(veps_made, n)
                nc.gpsimd.tensor_tensor(rstd[:, :], veps[:, :], power[:, :], ALU.pow).then_inc(made, 1)

            first = 1 if value is not None else 0
            if value is not None:
                pool.wait_ge(va_mv, 1)
                inverse_std(1, va_rstd)

            def next_value(b):
                if value is not None:
                    nc.gpsimd.tensor_copy(value_now[:, :], vb[:, b, :]).then_inc(value_now_made, 1)

            def take(b, slot, loads):
                pool.wait_ge(load[slot % 2], 16 * loads)
                if value is None:
                    nc.gpsimd.tensor_tensor(x[:, slot, :, :], x_raw[:, slot % 2, :, :],
                                            one[:, :].unsqueeze(2).broadcast_to([P, CB, C]),
                                            ALU.mult).then_inc(valued, 1)
                    return
                pool.wait_ge(value_now_made, b + 1)
                row = value_now[:, :].unsqueeze(1).broadcast_to([P, CB, C])
                nc.gpsimd.tensor_tensor(x[:, slot, :, :], x_raw[:, slot % 2, :, :], row,
                                        ALU.add).then_inc(valued, 1)

            def std_of(c):
                pool.wait_ge(mv_made, c + 1)
                need(xn_made, c)
                inverse_std(c + 1 + first, rstd_made)

            def step_of(c, s):
                pool.wait_ge(xt_made, c + 1)
                need(mix_made, 2 * c)
                nc.gpsimd.tensor_tensor(step[:, :, :], xt[:, s % 2, :, 1:N + 1], xt[:, s % 2, :, 0:N],
                                        ALU.subtract).then_inc(step_made, 1)

            if value is not None:
                pool.wait_ge(vb_made, BATCH)
            next_value(0)
            take(0, 0, 1)
            std_of(0)
            take(0, 1, 1)
            step_of(0, 0)
            std_of(1)
            take(0, 2, 2)

            def add_gated(c, s):
                pool.wait_ge(gated_made, 2 * (c + 1))
                need(stored[s % 2], 16 * (c // 2) if isinstance(c, int) else 8 * (c - s % 2))
                flat = lambda tile: tile.rearrange("p a c -> p (a c)")
                nc.gpsimd.tensor_tensor(flat(x_new[:, s % 2, :, :]), flat(x[:, s % SLOTS, :, :]),
                                        flat(gated[:, :, :]), ALU.add).then_inc(x_made, 1)

            def batch(pool, b):
                for s in range(CPB):
                    c = b * CPB + s
                    if remain(b, s, 1):
                        step_of(c + 1, s + 1)
                    if remain(b, s, 2):
                        std_of(c + 2)
                    if remain(b, s, 3) and s == 1 and value is not None:
                        pool.wait_ge(valued, CPB * (b + 1))
                    if before(b, s):
                        add_gated(c - 1, (s + SLOTS - 1) % SLOTS)
                    if remain(b, s, 3):
                        ahead = b + (s + 3) // CPB
                        if s == 1 and value is not None:
                            next_value(ahead)
                        need(x_made, c)
                        take(ahead, (s + 3) % SLOTS, 2 * ahead + (s + 3) % CPB // 2 + 1)
            over_batches(batch)(pool)
            add_gated(CHUNKS - 1, SLOTS - 1)

        @block.vector
        def _(dve):
            need = Need(dve)
            def moments(src, n, made):
                for j in range(CB):
                    last = nc.vector.bn_stats(stats[:, j, :], src[:, j, :])
                last.then_inc(stats_made, 1)
                dve.wait_ge(stats_made, n)
                nc.vector.memset(carrier[:, :], 0.0)
                for j in range(CB):
                    last = nc.vector.bn_aggr(mv[:, j, :], stats[:, j, :])
                last.then_inc(made, 1)

            def normalize(src, made):
                for j in range(CB):
                    last = nc.vector.tensor_scalar(xn[:, j, :], src[:, j, :], mv[:, j, 0:1], rstd[:, j:j + 1],
                                                   ALU.subtract, ALU.mult)
                last.then_inc(made, 1)

            first = 1 if value is not None else 0
            if value is not None:
                dve.wait_ge(value_in, 16 * BATCH)
                moments(xn, 1, va_mv)
                dve.wait_ge(va_rstd, 1)
                normalize(xn, va_xn)
            dve.wait_ge(consts, 16 * 5)
            dve.wait_ge(w_high, 1)
            nc.vector.tensor_tensor(w_l[:, :, :, :], w_raw[:, :, :, :], w_h[:, :, :, :].bitcast(F32),
                                    ALU.subtract).then_inc(w_low, 1)
            if value is not None:
                for b in range(BATCH):
                    dve.wait_ge(va_done, b + 1)
                    nc.vector.tensor_tensor(vb[:, b, :], v_ps[:, b // 2, (b % 2) * C:(b % 2 + 1) * C],
                                            ba[:, :], ALU.add).then_inc(vb_made, 1)

            def moments_of(c, slot):
                dve.wait_ge(valued, c + 1)
                need(rstd_made, c)
                need(xn_made, c)
                moments(x[:, slot, :, :], c + 1 + first, mv_made)

            def normalize_of(c, slot):
                dve.wait_ge(rstd_made, c + 1)
                need(t_done, c)
                if value is not None:
                    dve.wait_ge(va_t, BATCH)
                normalize(x[:, slot, :, :], xn_made)

            def mix_of(c, s):
                dve.wait_ge(step_made, c + 1)
                for n, m in enumerate((K, R)):
                    need(mixh_made, 2 * (c - 1) + n + 1)
                    need(mixl_made, 2 * (c - 1) + n + 1)
                    for k in range(CK):
                        last = nc.vector.scalar_tensor_tensor(
                            mix[:, m, k, :], step[:, k, :], mu[:, m, k:k + 1], xt[:, s % 2, k, 0:N],
                            ALU.mult, ALU.add)
                    last.then_inc(mix_made, 1)

            def mix_low(c, n):
                m = (K, R)[n]
                dve.wait_ge(mixh_made, 2 * c + n + 1)
                need((k_done, r_done)[n], 2 * c)
                nc.vector.tensor_tensor(mix_l[:, m, :, :], mix[:, m, :, :], mix_h[:, m, :, :].bitcast(F32),
                                        ALU.subtract).then_inc(mixl_made, 1)

            moments_of(0, 0)
            normalize_of(0, 0)
            moments_of(1, 1)
            mix_of(0, 0)
            normalize_of(1, 1)
            mix_low(0, 0)
            mix_low(0, 1)

            def act_low(c):
                for m in range(CK):
                    dve.wait_ge(acth_made, CK * c + m + 1)
                    need(v_done, 2 * c)
                    nc.vector.tensor_tensor(act_l[:, m, :], act[:, m, :], act_h[:, m, :].bitcast(F32),
                                            ALU.subtract).then_inc(actl_made, 1)

            def gate_value(c):
                need(x_made, c)
                for h in range(2):
                    dve.wait_ge(gate_made, 2 * c + h + 1)
                    dve.wait_ge(v_done, 2 * c + h + 1)
                    nc.vector.tensor_tensor(gated[:, h, :], v_ps[:, h, :], gate[:, h, :],
                                            ALU.mult).then_inc(gated_made, 1)

            def batch(dve, b):
                for s in range(CPB):
                    c = b * CPB + s
                    if remain(b, s, 2):
                        moments_of(c + 2, (s + 2) % SLOTS)
                    if remain(b, s, 1):
                        mix_of(c + 1, s + 1)
                    if before(b, s):
                        gate_value(c - 1)
                    if remain(b, s, 1):
                        mix_low(c + 1, 0)
                    if remain(b, s, 2):
                        normalize_of(c + 2, (s + 2) % SLOTS)
                    act_low(c)
                    if remain(b, s, 1):
                        mix_low(c + 1, 1)
            over_batches(batch)(dve)
            gate_value(CHUNKS - 1)

        @block.scalar
        def _(act_e):
            need = Need(act_e)
            if value is not None:
                act_e.dma_start(wa[:, :, :], value_wt.rearrange("(k p) c -> p k c", p=P)).then_inc(wa_in, 16)
                act_e.dma_start(ba[:, :], value_b.partition_broadcast(P)).then_inc(wa_in, 16)
            for w, ap in ((WR, wr_t), (WK, wk_t), (WV, wv_t)):
                act_e.dma_start(w_raw[:, w, :, :], ap.rearrange("(k p) c -> p k c", p=P)).then_inc(consts, 16)
            act_e.dma_start(mu[:, R, :], mu_r).then_inc(consts, 16)
            act_e.dma_start(mu[:, K, :], mu_k).then_inc(consts, 16)
            act_e.wait_ge(consts, 16 * 5)
            nc.scalar.activation(w_h[:, :, :, :], w_raw[:, :, :, :], ACT.Copy).then_inc(w_high, 1)
            if value is not None:
                act_e.wait_ge(va_t, BATCH)
                for b in range(BATCH):
                    nc.scalar.activation(mix[:, b // 2, :, (b % 2) * P:(b % 2 + 1) * P],
                                         t_ps[:, :, b * P:(b + 1) * P], ACT.Copy).then_inc(va_xt, 1)

            def transposed(c, s):
                act_e.wait_ge(t_done, c + 1)
                need(mix_made, 2 * (c - 1))
                if s % CPB == 0:
                    before = zero[:, :, :]
                    act_e.wait_ge(ident_made, 4)
                else:
                    before = xt[:, (s - 1) % 2, :, N:N + 1]
                    need(xt_made, c)
                nc.scalar.activation(xt[:, s % 2, :, 0:1], before, ACT.Copy)
                nc.scalar.activation(xt[:, s % 2, :, 1:N + 1], t_ps[:, :, :], ACT.Copy).then_inc(xt_made, 1)

            def mix_high(c, n):
                m = (K, R)[n]
                act_e.wait_ge(mix_made, 2 * c + n + 1)
                need((k_done, r_done)[n], 2 * c)
                nc.scalar.activation(mix_h[:, m, :, :], mix[:, m, :, :], ACT.Copy).then_inc(mixh_made, 1)

            def act_high(c, m):
                act_e.wait_ge(act_made, CK * c + m + 1)
                need(v_done, 2 * c)
                nc.scalar.activation(act_h[:, m, :], act[:, m, :], ACT.Copy).then_inc(acth_made, 1)

            transposed(0, 0)
            mix_high(0, 0)
            mix_high(0, 1)

            def batch(act_e, b):
                for s in range(CPB):
                    c = b * CPB + s
                    if remain(b, s, 1):
                        transposed(c + 1, s + 1)
                    for m in range(CK):
                        act_e.wait_ge(k_done, CK * c + m + 1)
                        need(act_made, CK * (c - 1) + m + 1)
                        nc.scalar.activation(relu[:, m, :], k_ps[:, m, :], ACT.Relu).then_inc(relu_made, 1)
                    for m in range(CK):
                        act_e.wait_ge(relu_made, CK * c + m + 1)
                        need(acth_made, CK * (c - 1) + m + 1)
                        need(actl_made, CK * (c - 1) + m + 1)
                        nc.scalar.activation(act[:, m, :], relu[:, m, :], ACT.Square).then_inc(act_made, 1)
                    if remain(b, s, 1):
                        mix_high(c + 1, 0)
                    for m in range(CK):
                        act_high(c, m)
                    if remain(b, s, 1):
                        mix_high(c + 1, 1)
                    for h in range(2):
                        act_e.wait_ge(r_done, 2 * c + h + 1)
                        need(gated_made, 2 * (c - 1) + h + 1)
                        nc.scalar.activation(gate[:, h, :], r_ps[:, h, :], ACT.Sigmoid).then_inc(gate_made, 1)
            over_batches(batch)(act_e)

        @block.tensor
        def _(pe):
            need = Need(pe)
            w_parts = (w_h, w_l)
            pe.wait_ge(ident_made, 4)
            if value is not None:
                pe.wait_ge(va_xn, 1)
                for b in range(BATCH):
                    for k in range(CK):
                        last = nc.tensor.transpose(t_ps[:, k, b * P:(b + 1) * P],
                                                   xn[:, b, k * P:(k + 1) * P], ident[:, :])
                    last.then_inc(va_t, 1)
                pe.wait_ge(va_xt, BATCH)
                pe.wait_ge(wa_in, 32)
                for b in range(BATCH):
                    for k in range(CK):
                        last = nc.tensor.matmul(v_ps[:, b // 2, (b % 2) * C:(b % 2 + 1) * C],
                                                mix[:, b // 2, k, (b % 2) * P:(b % 2 + 1) * P], wa[:, k, :],
                                                start=k == 0, stop=k == CK - 1)
                    if b % 2 == 1:
                        last.then_inc(va_done, 2)

            def transposes(c):
                pe.wait_ge(xn_made, c + 1)
                need(xt_made, c)
                for k in range(CK):
                    for j in range(CB):
                        last = nc.tensor.transpose(t_ps[:, k, j * P:(j + 1) * P],
                                                   xn[:, j, k * P:(k + 1) * P], ident[:, :])
                last.then_inc(t_done, 1)

            transposes(0)
            pe.wait_ge(w_low, 1)

            def values(c):
                pe.wait_ge(actl_made, CK * (c + 1))
                for h in range(2):
                    need(gated_made, 2 * (c - 1) + h + 1)
                    if value is not None and isinstance(c, int) and c == 0:
                        pe.wait_ge(vb_made, BATCH)
                    for j in range(2):
                        t = (2 * h + j) * P
                        for n, (wp, xp) in enumerate(TERMS):
                            for k in range(CK):
                                last = nc.tensor.matmul(
                                    v_ps[:, h, j * C:(j + 1) * C],
                                    (act_h, act_l)[xp][:, k, t:t + P], w_parts[wp][:, WV, k, :],
                                    start=n == 0 and k == 0, stop=n == 2 and k == CK - 1)
                    last.then_inc(v_done, 1)

            def batch(pe, b):
                for s in range(CPB):
                    c = b * CPB + s
                    if remain(b, s, 1):
                        transposes(c + 1)
                    pe.wait_ge(mixl_made, 2 * c + 1)
                    for m in range(CK):
                        need(relu_made, CK * (c - 1) + m + 1)
                        for n, (wp, xp) in enumerate(TERMS):
                            for k in range(CK):
                                last = nc.tensor.matmul(
                                    k_ps[:, m, :], w_parts[wp][:, WK, k, m * P:(m + 1) * P],
                                    (mix_h, mix_l)[xp][:, K, k, :],
                                    start=n == 0 and k == 0, stop=n == 2 and k == CK - 1)
                        last.then_inc(k_done, 1)
                    if before(b, s):
                        values(c - 1)
                    pe.wait_ge(mixl_made, 2 * c + 2)
                    for h in range(2):
                        need(gate_made, 2 * (c - 1) + h + 1)
                        for j in range(2):
                            t = (2 * h + j) * P
                            for n, (wp, xp) in enumerate(TERMS):
                                for k in range(CK):
                                    last = nc.tensor.matmul(
                                        r_ps[:, h, j * C:(j + 1) * C],
                                        (mix_h, mix_l)[xp][:, R, k, t:t + P], w_parts[wp][:, WR, k, :],
                                        start=n == 0 and k == 0, stop=n == 2 and k == CK - 1)
                        last.then_inc(r_done, 1)
            over_batches(batch)(pe)
            values(CHUNKS - 1)


def attention_phase(nc, sems, x_in, x_out, wq_t, wk_t, wv, wo_t, bq, bk, bv, bo, cos, sin, sin_neg):
    AHEAD = 2
    WCOLS = 8
    VE = HD + 1
    HI, LO = 0, 1
    TERMS = ((HI, HI), (HI, LO), (LO, HI))
    QC, KC, VC = 0, QKV, 2 * QKV

    def sem(what):
        return sems.enter_context(nc.semaphore(f"at_{what}"))

    with ExitStack() as mem:
        def sb(what, shape, dt=F32):
            return mem.enter_context(nc.sbuf_tensor(f"at_{what}", shape, dt))

        def pb(what, shape):
            return mem.enter_context(nc.psum_tensor(f"at_{what}", shape, F32))

        w_h = sb("w_h", [P, CK, 3 * QKV], F32R)
        w_l = sb("w_l", [P, CK, 3 * QKV], F32R)
        wo_h = sb("wo_h", [P, WCOLS, C], F32R)
        wo_l = sb("wo_l", [P, WCOLS, C], F32R)
        raw = sb("raw", [P, 2, CK * QKV])
        cos_sb = sb("cos", [P, BPB, HD // 2])
        sin_sb = sb("sin", [P, BPB, HD // 2])
        nsin_sb = sb("nsin", [P, BPB, HD // 2])
        bias = sb("bias", [HD, 2 * QKV], F32R)
        out_bias = sb("out_bias", [HD, C], F32R)
        ones = sb("ones", [HD, P], F32R)
        ones_raw = sb("ones_raw", [HD, P])
        bv_cols = sb("bv_cols", [P, WCOLS])
        bv_wide = sb("bv_wide", [P, WCOLS, HD])
        bo_sb = sb("bo_sb", [HD, C])
        row = sb("row", [HD, C])
        row_h = sb("row_h", [HD, C])
        wsum = sb("wsum", [P, WCOLS])
        v_down = sb("v_down", [P, WCOLS])
        v_up = sb("v_up", [P, WCOLS])
        masks = sb("masks", [P, 3, 2 * P])
        mask_even = sb("mask_even", [P, 2 * P])
        ident = sb("ident", [P, P])

        x_ln = sb("x_ln", [P, 2, C])
        x_res = sb("x_res", [P, 2, C])
        stats = sb("stats", [P, 6])
        mv = sb("mv", [P, 2])
        veps = sb("veps", [P, 1])
        power = sb("power", [P, 1])
        eps = sb("eps", [P, 1])
        carrier = sb("carrier", [P, 2])
        rstd = sb("rstd", [P, 1])
        xn = sb("xn", [P, C])
        xt_h = sb("xt_h", [P, 2, CK, P], F32R)
        xt_l = sb("xt_l", [P, 2, CK, P], F32R)
        by_cos = sb("by_cos", [P, 2, 512])
        by_sin = sb("by_sin", [P, 2, 512])
        k_rope = sb("k_rope", [P, 2, 512])
        q_rope = sb("q_rope", [P, 2, 512])
        qt_h = sb("qt_h", [P, WCOLS, P], F32R)
        qt_l = sb("qt_l", [P, WCOLS, P], F32R)
        kt_h = sb("kt_h", [P, WCOLS, 2, P], F32R)
        kt_l = sb("kt_l", [P, WCOLS, 2, P], F32R)
        v_h = sb("v_h", [P, 2, HEADS, VE], F16)
        v_l = sb("v_l", [P, 2, HEADS, HD], F16)
        masked = sb("masked", [P, 2, GROUP, 2 * P])
        top = sb("top", [P, 2, GROUP])
        shift = sb("shift", [P, 2, GROUP])
        prob = sb("prob", [P, 2, GROUP, 2 * P])
        pt_h = sb("pt_h", [P, 2, 2, 512], F16)
        pt_l = sb("pt_l", [P, 2, 2, 512], F16)
        inv = sb("inv", [P, GROUP, 1])
        ctx = sb("ctx", [P, QKV])
        ct_h = sb("ct_h", [P, WCOLS, P], F32R)
        ct_l = sb("ct_l", [P, WCOLS, P], F32R)

        s_ps = pb("s_ps", [P, 2, 512])
        pr_ps = pb("pr_ps", [P, 2, 512])
        c_ps = pb("c_ps", [P, 512])
        tb = [pb(f"tb{n}", [P, 512]) for n in range(3)]

        tab_in = sem("tab_in")
        raw_in = [sem("raw_in0"), sem("raw_in1")]
        made = sem("made")
        w_high = sem("w_high")
        w_low = sem("w_low")
        w_free = sem("w_free")
        v_bound = sem("v_bound")
        v_chain = sem("v_chain")
        v_scaled = sem("v_scaled")
        wo_scaled = sem("wo_scaled")
        bv_made = sem("bv_made")
        ob_done = sem("ob_done")
        row_made = sem("row_made")
        rowh_made = sem("rowh_made")
        brow_h = sem("brow_h")
        brow_l = sem("brow_l")
        wt_done = sem("wt_done")
        wt_high = sem("wt_high")
        wt_low = sem("wt_low")

        ln_in = [sem("ln_in0"), sem("ln_in1")]
        res_in = [sem("res_in0"), sem("res_in1")]
        stored = [sem("stored0"), sem("stored1")]
        stats_made = sem("stats_made")
        mv_made = sem("mv_made")
        veps_made = sem("veps_made")
        rstd_made = sem("rstd_made")
        xn_made = sem("xn_made")
        tx_done = sem("tx_done")
        xt_high = sem("xt_high")
        xt_low = sem("xt_low")
        k_done = sem("k_done")
        q_done = sem("q_done")
        k_by = sem("k_by")
        q_by = sem("q_by")
        k_roped = sem("k_roped")
        q_roped = sem("q_roped")
        tk_done = sem("tk_done")
        tq_done = sem("tq_done")
        kt_high = sem("kt_high")
        kt_low = sem("kt_low")
        qt_high = sem("qt_high")
        qt_low = sem("qt_low")
        vp_done = sem("vp_done")
        v_high = sem("v_high")
        v_low = sem("v_low")
        s_done = sem("s_done")
        top_made = sem("top_made")
        shift_made = sem("shift_made")
        p_made = sem("p_made")
        pt_done = sem("pt_done")
        pt_high = sem("pt_high")
        pt_low = sem("pt_low")
        pv_done = sem("pv_done")
        inv_made = sem("inv_made")
        ctx_made = sem("ctx_made")
        tc_done = sem("tc_done")
        ct_high = sem("ct_high")
        ct_low = sem("ct_low")
        wo_done = sem("wo_done")
        x_made = sem("x_made")
        mask_made = sem("mask_made")

        TURNS = [("pt", 0), ("pt", 1), ("tc", 0), ("tc", 1), ("pt", 2), ("pt", 3), ("tx", 0), ("tk", 0),
                 ("tq", 0), ("pt", 4), ("pt", 5), ("tk", 1), ("tq", 1), ("pt", 6), ("pt", 7)]
        LOW = {"pt": pt_low, "tc": ct_low, "tk": kt_low, "tq": qt_low, "tx": xt_low}

        def present(what, i):
            if not isinstance(i, int):
                return True
            return {"pt": 0 <= i < NBLK, "tc": i >= 1, "tk": 0 <= i < NBLK - 1, "tq": 0 <= i < NBLK - 1,
                    "tx": 0 <= i < NBLK - AHEAD}[what]

        def low_count(what, i, n):
            return {"pt": 2 * NG * i + n + 1, "tc": 2 * (i - 1) + n + 1, "tk": 2 * (i + 1) + n + 1,
                    "tq": 2 * (i + 1) + n + 1, "tx": i + AHEAD + 1}[what]

        def turn_bank(what, n):
            return tb[TURNS.index((what, n)) % 3]

        def wait_turn(pe, what, n, i):
            at = TURNS.index((what, n)) - 3
            step = i
            while True:
                if at < 0:
                    at, step = at + len(TURNS), step - 1
                if isinstance(step, int) and step < 0:
                    pe.wait_ge(qt_low, 2)
                    pe.wait_ge(xt_low, AHEAD)
                    return
                if present(TURNS[at][0], step):
                    pe.wait_ge(LOW[TURNS[at][0]], low_count(TURNS[at][0], step, TURNS[at][1]))
                    return
                at -= 3

        def count(j, q, per=1):
            return 16 * per * (j + q // 2 + 1)

        MADE = 3 + 6 + 7 + 1
        block = mem.enter_context(nc.Block())

        def over_pairs(body):
            def run(eng):
                body(eng, 0)
                with eng.Fori(1, NBLK // 2 - 1) as j:
                    body(eng, j)
                body(eng, NBLK // 2 - 1)
            return run

        def exists(j, q):
            return not isinstance(j, int) or 0 <= 2 * j + q < NBLK

        @block.sync
        def _(sp):
            need = Need(sp)
            for s in range(AHEAD):
                sp.dma_start(x_ln[:, s, :], x_in[:, s, :]).then_inc(ln_in[s], 16)

            def weights(n, ap):
                need(w_free, n - 1)
                sp.dma_start(raw[:, n % 2, :].rearrange("p (a b) -> p a b", a=ap.shape[0] // P),
                             ap.rearrange("(k p) c -> p k c", p=P)).then_inc(raw_in[n % 2], 16)
            weights(0, wk_t)
            weights(1, wq_t)
            tables = [(cos_sb[:, :, :], cos), (sin_sb[:, :, :], sin), (nsin_sb[:, :, :], sin_neg),
                      (bv_cols[:, :], bv), (bo_sb[:, :], bo.partition_broadcast(HD)),
                      (masked[0:HD, 0, :, :].rearrange("p a b -> p (a b)"), bq.partition_broadcast(HD)),
                      (masked[0:HD, 1, :, :].rearrange("p a b -> p (a b)"), bk.partition_broadcast(HD))]
            for dst, src in tables:
                sp.dma_start(dst, src).then_inc(tab_in, 16)
            weights(2, wv)
            weights(3, wo_t)

            def pair(sp, j):
                for s in range(2):
                    i = 2 * j + s
                    if exists(j, s + AHEAD):
                        sp.wait_ge(xn_made, i + 1)
                        sp.dma_start(x_ln[:, s, :], x_in[:, i + AHEAD, :]).then_inc(ln_in[s], 16)
                    need(stored[s], count(j, s) - 16)
                    sp.dma_start(x_res[:, s, :], x_in[:, i, :]).then_inc(res_in[s], 16)
                    if exists(j, s - 1):
                        sp.wait_ge(x_made, i)
                        sp.dma_start(x_out[:, i - 1, :], x_res[:, 1 - s, :]).then_inc(stored[1 - s], 16)
            over_pairs(pair)(sp)
            sp.wait_ge(x_made, NBLK)
            sp.dma_start(x_out[:, NBLK - 1, :], x_res[:, 1, :]).then_inc(stored[1], 16)
            for s in range(2):
                sp.wait_ge(stored[s], 16 * NBLK // 2)

        @block.gpsimd
        def _(pool):
            need = Need(pool)
            nc.gpsimd.memset(power[:, :], -0.5)
            nc.gpsimd.memset(eps[:, :], EPS)
            nc.gpsimd.memset(ones_raw[:, :], 1.0)
            nc.gpsimd.memset(masks[:, :, :], 0.0).then_inc(made, 1)
            identity(nc, pool, ident, made, 2)
            past = dict(compare_op=ALU.is_ge, fill=MASKED, base=0, pattern=[[1, P]], channel_multiplier=-1)
            own = dict(compare_op=ALU.is_ge, fill=MASKED, base=0, pattern=[[-1, P]], channel_multiplier=1)
            nc.gpsimd.memset(masks[:, 0, P:2 * P], MASKED).then_inc(made, 1)
            for m, half, kind in ((0, 0, own), (1, 0, own), (1, 1, past), (2, 0, past), (2, 1, own)):
                part = masks[:, m, half * P:(half + 1) * P]
                nc.gpsimd.affine_select(out=part, in_=part, **kind).then_inc(made, 1)
            nc.gpsimd.memset(bias[:, :].bitcast(F32), 0.0).then_inc(made, 1)
            nc.gpsimd.memset(out_bias[:, :].bitcast(F32), 0.0).then_inc(made, 1)
            nc.gpsimd.memset(kt_h[:, :, 1, :].bitcast(F32), 0.0).then_inc(made, 1)
            nc.gpsimd.memset(kt_l[:, :, 1, :].bitcast(F32), 0.0).then_inc(made, 1)
            nc.gpsimd.memset(v_h[:, 1, :, 0:HD], 0.0).then_inc(made, 1)
            nc.gpsimd.memset(v_h[:, :, :, HD:VE], 1.0).then_inc(made, 1)
            nc.gpsimd.memset(v_l[:, 1, :, :], 0.0).then_inc(made, 1)
            pool.wait_ge(made, MADE - 1)
            nc.gpsimd.tensor_copy(mask_even[:, :], masks[:, 0, :]).then_inc(made, 1)

            def inverse_std(t):
                pool.wait_ge(mv_made, t + 1)
                need(xn_made, t)
                nc.gpsimd.tensor_tensor(veps[:, :], mv[:, 1:2], eps[:, :], ALU.add).then_inc(veps_made, 1)
                pool.wait_ge(veps_made, t + 1)
                nc.gpsimd.tensor_tensor(rstd[:, :], veps[:, :], power[:, :], ALU.pow).then_inc(rstd_made, 1)

            def rope(f, ch, by, rope_sb, roped, transposed):
                pool.wait_ge(by, 2 * f + ch + 1)
                need(transposed, 2 * (f - 1) + ch + 1)
                nc.gpsimd.tensor_tensor(rope_sb[:, ch, :], by_cos[:, ch, :], by_sin[:, ch, :],
                                        ALU.add).then_inc(roped, 1)

            for t in range(AHEAD):
                inverse_std(t)
            for ch in range(2):
                rope(0, ch, k_by, k_rope, k_roped, tk_done)
            for ch in range(2):
                rope(0, ch, q_by, q_rope, q_roped, tq_done)
            for ch in range(2):
                rope(1, ch, k_by, k_rope, k_roped, tk_done)

            def pair(pool, j):
                for s in range(2):
                    i = 2 * j + s
                    if exists(j, s + 2):
                        inverse_std(i + 2)
                    if exists(j, s + 1):
                        for ch in range(2):
                            rope(i + 1, ch, q_by, q_rope, q_roped, tq_done)
                    if exists(j, s + 2):
                        for ch in range(2):
                            rope(i + 2, ch, k_by, k_rope, k_roped, tk_done)
            over_pairs(pair)(pool)

        @block.vector
        def _(dve):
            need = Need(dve)

            def moments(t, slot, loaded):
                dve.wait_ge(ln_in[slot], loaded)
                nc.vector.bn_stats(stats[:, :], x_ln[:, slot, :]).then_inc(stats_made, 1)
                dve.wait_ge(stats_made, t + 1)
                need(rstd_made, t)
                nc.vector.memset(carrier[:, 0:1], 0.0)
                nc.vector.bn_aggr(mv[:, :], stats[:, :]).then_inc(mv_made, 1)

            def normalize(t, slot):
                dve.wait_ge(rstd_made, t + 1)
                need(tx_done, t)
                nc.vector.tensor_scalar(xn[:, :], x_ln[:, slot, :], mv[:, 0:1], rstd[:, :],
                                        ALU.subtract, ALU.mult).then_inc(xn_made, 1)

            def low(out, src, high, sem_, dt=F32):
                high = high.bitcast(F32) if dt is F32 else high
                nc.vector.tensor_tensor(out, src, high, ALU.subtract).then_inc(sem_, 1)

            def xt_low_of(t, slot, bank):
                dve.wait_ge(xt_high, t + 1)
                low(xt_l[:, slot, :, :], bank[:, 0:C].rearrange("p (k t) -> p k t", k=CK),
                    xt_h[:, slot, :, :], xt_low)

            def ropes(f, ch, n, done, by, before):
                dve.wait_ge(done, 2 * f + ch + 1)
                need(*before)
                src = pr_ps[:, ch, :].rearrange("p (h d) -> p h d", d=HD // 2)
                c = cos_sb[:, n, :].unsqueeze(1).broadcast_to([P, 16, HD // 2])
                nc.vector.tensor_tensor(by_cos[:, ch, :].rearrange("p (h d) -> p h d", d=HD // 2), src, c,
                                        ALU.mult)
                halves = pr_ps[:, ch, :].rearrange("p (h e d) -> p e h d", e=2, d=HD // 2)
                out = by_sin[:, ch, :].rearrange("p (h e d) -> p e h d", e=2, d=HD // 2)
                for e, table in enumerate((nsin_sb, sin_sb)):
                    t = table[:, n, :].unsqueeze(1).broadcast_to([P, 8, HD // 2])
                    last = nc.vector.tensor_tensor(out[:, e], halves[:, 1 - e], t, ALU.mult)
                last.then_inc(by, 1)

            def k_products(f, ch, n):
                ropes(f, ch, n, k_done, k_by, (q_roped, 2 * (f - 1) + ch + 1))

            def q_products(f, ch, n):
                ropes(f, ch, n, q_done, q_by, (k_roped, 2 * f + ch + 1))

            def kt_low_of(f, b, slot, bank):
                dve.wait_ge(kt_high, 2 * f + b + 1)
                low(kt_l[:, 4 * b:4 * b + 4, slot, :], bank[:, :].rearrange("p (k t) -> p k t", k=4),
                    kt_h[:, 4 * b:4 * b + 4, slot, :], kt_low)

            def qt_low_of(f, b, bank):
                dve.wait_ge(qt_high, 2 * f + b + 1)
                low(qt_l[:, 4 * b:4 * b + 4, :], bank[:, :].rearrange("p (k t) -> p k t", k=4),
                    qt_h[:, 4 * b:4 * b + 4, :], qt_low)

            for n, col in ((0, KC), (1, QC)):
                dve.wait_ge(w_high, n + 1)
                for k in range(CK):
                    last = nc.vector.tensor_tensor(
                        w_l[:, k, col:col + QKV], raw[:, n, k * QKV:(k + 1) * QKV],
                        w_h[:, k, col:col + QKV].bitcast(F32), ALU.subtract)
                last.then_inc(w_free, 1)
            for t in range(AHEAD):
                moments(t, t, 16)
                normalize(t, t)
                xt_low_of(t, t, tb[t])
            dve.wait_ge(brow_h, 1)
            b_raw = masked[0:HD, :, :, :].rearrange("p e a b -> p (e a b)")
            b_high = prob[0:HD, :, :, :].rearrange("p e a b -> p (e a b)")
            nc.vector.tensor_tensor(bias[32:33, :], b_raw[32:33, :], b_high[32:33, :],
                                    ALU.subtract).then_inc(brow_l, 1)
            dve.wait_ge(raw_in[0], 32)
            wv_raw = raw[:, 0, :].rearrange("p (a c) -> p a c", a=WCOLS)
            nc.vector.tensor_reduce(wsum[:, :], wv_raw, AX.X, ALU.add,
                                    apply_absolute_value=True).then_inc(v_chain, 1)
            dve.wait_ge(v_chain, 1)
            nc.vector.tensor_scalar(v_down[:, :], wsum[:, :], float(np.sqrt(C)) / V_TOP, 1e-30, ALU.mult,
                                    ALU.max).then_inc(v_chain, 1)
            dve.wait_ge(v_chain, 2)
            nc.vector.reciprocal(v_up[:, :], v_down[:, :]).then_inc(v_chain, 1)
            dve.wait_ge(v_chain, 3)
            for a in range(WCOLS):
                last = nc.vector.tensor_scalar(wv_raw[:, a, :], wv_raw[:, a, :], v_up[:, a:a + 1], None, ALU.mult)
            last.then_inc(v_scaled, 1)
            dve.wait_ge(tab_in, 16 * 7)
            nc.vector.tensor_copy(bv_wide[:, :, :], bv_cols[:, :].unsqueeze(2).broadcast_to([P, WCOLS, HD]))\
                .then_inc(bv_made, 1)
            dve.wait_ge(ob_done, 1)
            nc.vector.tensor_tensor(row[:, :], c_ps[0:HD, 0:C], bo_sb[:, :], ALU.add).then_inc(row_made, 1)
            dve.wait_ge(rowh_made, 1)
            nc.vector.tensor_tensor(out_bias[32:33, :], row[32:33, :], row_h[32:33, :],
                                    ALU.subtract).then_inc(rowh_made, 1)
            wo_raw = raw[:, 1, :].rearrange("p (a c) -> p a c", a=WCOLS)
            for a in range(WCOLS):
                last = nc.vector.tensor_scalar(wo_raw[:, a, :], wo_raw[:, a, :], v_down[:, a:a + 1], None, ALU.mult)
            last.then_inc(wo_scaled, 1)
            dve.wait_ge(w_high, 3)
            nc.vector.tensor_tensor(wo_l[:, :, :], wo_raw, wo_h[:, :, :].bitcast(F32),
                                    ALU.subtract).then_inc(w_low, 1)
            for n in range(4):
                dve.wait_ge(wt_high, n + 1)
                k, half = divmod(n, 2)
                cols = VC + half * 512
                nc.vector.tensor_tensor(w_l[:, k, cols:cols + 512], (pr_ps[:, 0, :], pr_ps[:, 1, :])[n % 2],
                                        w_h[:, k, cols:cols + 512].bitcast(F32), ALU.subtract).then_inc(wt_low, 1)
            dve.wait_ge(made, MADE)
            for ch in range(2):
                k_products(0, ch, 0)
            for ch in range(2):
                q_products(0, ch, 0)
            for b in range(2):
                kt_low_of(0, b, 0, tb[b])
            for b in range(2):
                qt_low_of(0, b, tb[(b + 2) % 3])
            for ch in range(2):
                k_products(1, ch, 1)

            def tops(bi, odd, g):
                dve.wait_ge(s_done, NG * bi + g + 1)
                need(p_made, NG * bi + g - 1)
                nc.vector.memset(carrier[:, 1:2], 0.0)
                for h in range(GROUP):
                    last = nc.vector.tensor_tensor_reduce(
                        out=masked[:, g % 2, h, :], in0=s_ps[:, h % 2, (h // 2) * 2 * P:(h // 2 + 1) * 2 * P],
                        in1=masks[:, 2, :] if odd else mask_even[:, :], scale=1.0, scalar=-3e38,
                        op0=ALU.add, op1=ALU.max, accum_out=top[:, g % 2, h:h + 1])
                last.then_inc(top_made, 1)
                dve.wait_ge(top_made, NG * bi + g + 1)
                nc.vector.tensor_scalar(shift[:, g % 2, :], top[:, g % 2, :], -SCALE, None,
                                        ALU.mult).then_inc(shift_made, 1)

            tops(0, False, 0)

            def pair(dve, j):
                for s in range(2):
                    i = 2 * j + s
                    front, ahead = exists(j, s + 1), exists(j, s + 2)

                    def context(bi, g):
                        dve.wait_ge(pv_done, NG * bi + g + 1)
                        src = c_ps[:, 0:GROUP * VE].rearrange("p (h d) -> p h d", d=VE)
                        nc.vector.reciprocal(inv[:, :, :], src[:, :, HD:VE]).then_inc(inv_made, 1)
                        dve.wait_ge(inv_made, NG * bi + g + 1)
                        nc.vector.tensor_tensor(
                            ctx[:, g * GROUP * HD:(g + 1) * GROUP * HD].rearrange("p (h d) -> p h d", d=HD),
                            src[:, :, 0:HD], inv[:, :, :].broadcast_to([P, GROUP, HD]),
                            ALU.mult).then_inc(ctx_made, 1)

                    def pt_low_of(g):
                        for half in range(2):
                            n = 2 * g + half
                            dve.wait_ge(pt_high, 2 * NG * i + n + 1)
                            low(pt_l[:, g % 2, half, :], turn_bank("pt", n)[:, :], pt_h[:, g % 2, half, :],
                                pt_low, F16)

                    tops(i, s, 1)
                    if ahead:
                        moments(i + 2, s, count(j, s + 2))
                    if exists(j, s - 1):
                        context(i - 1, NG - 1)
                    for ch in range(2):
                        dve.wait_ge(v_high, 2 * i + ch + 1)
                        nc.vector.tensor_tensor(v_l[:, s, 8 * ch:8 * ch + 8, :],
                                                pr_ps[:, ch, :].rearrange("p (h d) -> p h d", d=HD),
                                                v_h[:, s, 8 * ch:8 * ch + 8, 0:HD], ALU.subtract).then_inc(v_low, 1)
                    pt_low_of(0)
                    tops(i, s, 2)
                    if ahead:
                        normalize(i + 2, s)
                    if exists(j, s - 1):
                        for b in range(2):
                            dve.wait_ge(ct_high, 2 * (i - 1) + b + 1)
                            low(ct_l[:, 4 * b:4 * b + 4, :],
                                turn_bank("tc", b)[:, :].rearrange("p (k t) -> p k t", k=4),
                                ct_h[:, 4 * b:4 * b + 4, :], ct_low)
                    if front:
                        for ch in range(2):
                            q_products(i + 1, ch, (i + 1) % BPB)
                    context(i, 0)
                    pt_low_of(1)
                    tops(i, s, 3)
                    if ahead:
                        xt_low_of(i + 2, s, turn_bank("tx", 0))
                    if front:
                        kt_low_of(i + 1, 0, 1 - s, turn_bank("tk", 0))
                        qt_low_of(i + 1, 0, turn_bank("tq", 0))
                    if exists(j, s - 1):
                        dve.wait_ge(wo_done, i)
                        dve.wait_ge(res_in[1 - s], count(j, s - 1))
                        nc.vector.tensor_tensor(x_res[:, 1 - s, :], c_ps[:, 0:C], x_res[:, 1 - s, :],
                                                ALU.add).then_inc(x_made, 1)
                    context(i, 1)
                    pt_low_of(2)
                    if front:
                        if s == 1:
                            sel = ((j + 1) % (BPB // 2) + BPB // 2 - 1) // (BPB // 2)
                            nc.vector.tensor_copy(mask_even[:, :], masks[:, sel, :]).then_inc(mask_made, 1)
                            dve.wait_ge(mask_made, j + 1)
                        tops(i + 1, 1 - s, 0)
                        kt_low_of(i + 1, 1, 1 - s, turn_bank("tk", 1))
                        qt_low_of(i + 1, 1, turn_bank("tq", 1))
                    if ahead:
                        for ch in range(2):
                            k_products(i + 2, ch, (i + 2) % BPB)
                    context(i, 2)
                    pt_low_of(3)
            over_pairs(pair)(dve)
            dve.wait_ge(pv_done, NG * NBLK)
            src = c_ps[:, 0:GROUP * VE].rearrange("p (h d) -> p h d", d=VE)
            nc.vector.reciprocal(inv[:, :, :], src[:, :, HD:VE]).then_inc(inv_made, 1)
            dve.wait_ge(inv_made, NG * NBLK)
            nc.vector.tensor_tensor(ctx[:, 3 * GROUP * HD:QKV].rearrange("p (h d) -> p h d", d=HD),
                                    src[:, :, 0:HD], inv[:, :, :].broadcast_to([P, GROUP, HD]),
                                    ALU.mult).then_inc(ctx_made, 1)
            for b in range(2):
                dve.wait_ge(ct_high, 2 * (NBLK - 1) + b + 1)
                low(ct_l[:, 4 * b:4 * b + 4, :], turn_bank("tc", b)[:, :].rearrange("p (k t) -> p k t", k=4),
                    ct_h[:, 4 * b:4 * b + 4, :], ct_low)
            dve.wait_ge(wo_done, NBLK)
            dve.wait_ge(res_in[1], 16 * NBLK // 2)
            nc.vector.tensor_tensor(x_res[:, 1, :], c_ps[:, 0:C], x_res[:, 1, :], ALU.add).then_inc(x_made, 1)

        @block.scalar
        def _(act):
            def copy(out, in_, sem_):
                nc.scalar.activation(out, in_, ACT.Copy).then_inc(sem_, 1)

            def xt_high_of(t, slot, bank):
                act.wait_ge(tx_done, t + 1)
                copy(xt_h[:, slot, :, :], bank[:, 0:C].rearrange("p (k t) -> p k t", k=CK), xt_high)

            def kt_high_of(f, b, slot, bank):
                act.wait_ge(tk_done, 2 * f + b + 1)
                copy(kt_h[:, 4 * b:4 * b + 4, slot, :], bank[:, :].rearrange("p (k t) -> p k t", k=4), kt_high)

            def qt_high_of(f, b, bank):
                act.wait_ge(tq_done, 2 * f + b + 1)
                copy(qt_h[:, 4 * b:4 * b + 4, :], bank[:, :].rearrange("p (k t) -> p k t", k=4), qt_high)

            for n, col in ((0, KC), (1, QC)):
                act.wait_ge(raw_in[n], 16)
                copy(w_h[:, :, col:col + QKV], raw[:, n, :].rearrange("p (k c) -> p k c", k=CK), w_high)
            for t in range(AHEAD):
                xt_high_of(t, t, tb[t])
            act.wait_ge(made, MADE)
            nc.scalar.activation(ones[:, :], ones_raw[:, :], ACT.Copy)
            act.wait_ge(tab_in, 16 * 7)
            b_raw = masked[0:HD, :, :, :].rearrange("p e a b -> p (e a b)")
            b_high = prob[0:HD, :, :, :].rearrange("p e a b -> p (e a b)")
            nc.scalar.activation(b_high.bitcast(F32R), b_raw, ACT.Copy)
            copy(bias[0:1, :], b_raw[0:1, :], brow_h)
            act.wait_ge(row_made, 1)
            nc.scalar.activation(row_h[:, :].bitcast(F32R), row[:, :], ACT.Copy)
            copy(out_bias[0:1, :], row[0:1, :], rowh_made)
            act.wait_ge(wo_scaled, 1)
            copy(wo_h[:, :, :], raw[:, 1, :].rearrange("p (a c) -> p a c", a=WCOLS), w_high)
            for n in range(4):
                act.wait_ge(wt_done, n + 1)
                k, half = divmod(n, 2)
                copy(w_h[:, k, VC + half * 512:VC + half * 512 + 512], pr_ps[:, n % 2, :], wt_high)
            for b in range(2):
                kt_high_of(0, b, 0, tb[b])
            for b in range(2):
                qt_high_of(0, b, tb[(b + 2) % 3])

            def exps(bi, g):
                act.wait_ge(shift_made, NG * bi + g + 1)
                Need(act)(pt_done, 2 * (NG * bi + g - 1))
                for h in range(GROUP):
                    last = nc.scalar.activation(prob[:, g % 2, h, :], masked[:, g % 2, h, :], ACT.Exp,
                                                bias=shift[:, g % 2, h:h + 1], scale=SCALE)
                last.then_inc(p_made, 1)

            exps(0, 0)

            def pair(act, j):
                for s in range(2):
                    i = 2 * j + s
                    front, ahead = exists(j, s + 1), exists(j, s + 2)

                    def pt_high_of(g):
                        for half in range(2):
                            n = 2 * g + half
                            act.wait_ge(pt_done, 2 * NG * i + n + 1)
                            copy(pt_h[:, g % 2, half, :], turn_bank("pt", n)[:, :], pt_high)

                    exps(i, 1)
                    for ch in range(2):
                        act.wait_ge(vp_done, 2 * i + ch + 1)
                        Need(act)(pv_done, NG * i if exists(j, s - 1) else 0)
                        copy(v_h[:, s, 8 * ch:8 * ch + 8, 0:HD],
                             pr_ps[:, ch, :].rearrange("p (h d) -> p h d", d=HD), v_high)
                    pt_high_of(0)
                    if exists(j, s - 1):
                        for b in range(2):
                            act.wait_ge(tc_done, 2 * (i - 1) + b + 1)
                            copy(ct_h[:, 4 * b:4 * b + 4, :],
                                 turn_bank("tc", b)[:, :].rearrange("p (k t) -> p k t", k=4), ct_high)
                    exps(i, 2)
                    pt_high_of(1)
                    if ahead:
                        xt_high_of(i + 2, s, turn_bank("tx", 0))
                    if front:
                        kt_high_of(i + 1, 0, 1 - s, turn_bank("tk", 0))
                        qt_high_of(i + 1, 0, turn_bank("tq", 0))
                    exps(i, 3)
                    pt_high_of(2)
                    if front:
                        kt_high_of(i + 1, 1, 1 - s, turn_bank("tk", 1))
                        qt_high_of(i + 1, 1, turn_bank("tq", 1))
                        exps(i + 1, 0)
                    pt_high_of(3)
            over_pairs(pair)(act)
            for b in range(2):
                act.wait_ge(tc_done, 2 * (NBLK - 1) + b + 1)
                copy(ct_h[:, 4 * b:4 * b + 4, :], turn_bank("tc", b)[:, :].rearrange("p (k t) -> p k t", k=4),
                     ct_high)

        @block.tensor
        def _(pe):
            need = Need(pe)
            w = (w_h, w_l)
            wo = (wo_h, wo_l)
            xt = (xt_h, xt_l)

            def transpose_x(t, bank):
                pe.wait_ge(xn_made, t + 1)
                for k in range(CK):
                    last = nc.tensor.transpose(bank[:, k * P:(k + 1) * P], xn[:, k * P:(k + 1) * P], ident[:, :])
                last.then_inc(tx_done, 1)

            def project(slot, ch, col, done, bias_col=None):
                if bias_col is not None:
                    nc.tensor.matmul(pr_ps[:, ch, :], ones[:, :], bias[:, bias_col:bias_col + 512],
                                     start=True, stop=False)
                for n, (xp, wp) in enumerate(TERMS):
                    for k in range(CK):
                        last = nc.tensor.matmul(pr_ps[:, ch, :], xt[xp][:, slot, k, :], w[wp][:, k, col:col + 512],
                                                start=bias_col is None and n == 0 and k == 0,
                                                stop=n == 2 and k == CK - 1)
                last.then_inc(done, 1)

            def keys(f, slot):
                for ch in range(2):
                    need(q_by, 2 * (f - 1) + ch + 1)
                    project(slot, ch, KC + ch * 512, k_done, QKV + ch * 512)

            def queries(slot, read, read_count):
                for ch in range(2):
                    pe.wait_ge(read, read_count + ch + 1)
                    project(slot, ch, QC + ch * 512, q_done, ch * 512)

            def transpose_rope(f, b, src, roped, bank, done):
                pe.wait_ge(roped, 2 * f + b + 1)
                for a in range(4):
                    last = nc.tensor.transpose(bank[:, a * P:(a + 1) * P], src[:, b, a * P:(a + 1) * P], ident[:, :])
                last.then_inc(done, 1)

            def output(bi):
                pe.wait_ge(ct_low, 2 * (bi + 1))
                nc.tensor.matmul(c_ps[:, 0:C], ones[:, :], out_bias[:, :], start=True, stop=False)
                for n, (xp, wp) in enumerate(TERMS):
                    for a in range(WCOLS):
                        last = nc.tensor.matmul(c_ps[:, 0:C], (ct_h, ct_l)[xp][:, a, :], wo[wp][:, a, :],
                                                start=False, stop=n == 2 and a == WCOLS - 1)
                last.then_inc(wo_done, 1)

            def values_product(g):
                for h in range(GROUP):
                    head = g * GROUP + h
                    out = c_ps[:, h * VE:h * VE + VE]
                    for slot in range(2):
                        ph = pt_h[:, g % 2, h // 2, ((h % 2) * 2 + slot) * P:((h % 2) * 2 + slot + 1) * P]
                        pl = pt_l[:, g % 2, h // 2, ((h % 2) * 2 + slot) * P:((h % 2) * 2 + slot + 1) * P]
                        nc.tensor.matmul(out, ph, v_h[:, slot, head, :], start=slot == 0, stop=False)
                        nc.tensor.matmul(out[:, 0:HD], ph, v_l[:, slot, head, :], start=False, stop=False)
                        last = nc.tensor.matmul(out, pl, v_h[:, slot, head, :], start=False, stop=slot == 1)
                last.then_inc(pv_done, 1)

            pe.wait_ge(made, 3)
            for t in range(AHEAD):
                transpose_x(t, tb[t])
            pe.wait_ge(bv_made, 1)
            pe.wait_ge(raw_in[1], 32)
            for a in range(WCOLS):
                last = nc.tensor.matmul(c_ps[0:HD, 0:C], bv_wide[:, a, :],
                                        raw[:, 1, a * C:(a + 1) * C], start=a == 0, stop=a == WCOLS - 1)
            last.then_inc(ob_done, 1)
            pe.wait_ge(v_scaled, 1)
            for n in range(4):
                k, half = divmod(n, 2)
                need(wt_low, n - 1)
                for a in range(4):
                    o = 4 * half + a
                    last = nc.tensor.transpose(pr_ps[:, n % 2, a * P:(a + 1) * P],
                                               raw[:, 0, o * C + k * P:o * C + (k + 1) * P], ident[:, :])
                last.then_inc(wt_done, 1)
            pe.wait_ge(w_free, 2)
            pe.wait_ge(w_low, 1)
            pe.wait_ge(wt_low, 4)
            pe.wait_ge(xt_low, AHEAD)
            pe.wait_ge(brow_l, 1)
            pe.wait_ge(rowh_made, 2)
            keys(0, 0)
            queries(0, k_by, 0)
            for b in range(2):
                transpose_rope(0, b, k_rope, k_roped, tb[b], tk_done)
            for b in range(2):
                if b == 1:
                    pe.wait_ge(kt_low, 1)
                transpose_rope(0, b, q_rope, q_roped, tb[(b + 2) % 3], tq_done)

            def scores(bi, g):
                pe.wait_ge(qt_low, 2 * bi + g // 2 + 1)
                pe.wait_ge(kt_low, 2 * bi + g // 2 + 1)
                need(top_made, NG * bi + g)
                for a in range(2):
                    for n, (qp, kp) in enumerate(TERMS):
                        for e in range(2):
                            rows = slice(e * HD, (e + 1) * HD)
                            last = nc.tensor.matmul(
                                s_ps[:, e, a * 2 * P:(a + 1) * 2 * P],
                                (qt_h, qt_l)[qp][rows, 2 * g + a, :],
                                (kt_h, kt_l)[kp][rows, 2 * g + a, :, :].rearrange("p s t -> p (s t)"),
                                start=n == 0, stop=n == 2)
                last.then_inc(s_done, 1)

            scores(0, 0)
            keys(1, 1)

            def pair(pe, j):
                for s in range(2):
                    i = 2 * j + s
                    front, ahead = exists(j, s + 1), exists(j, s + 2)

                    def transpose_prob(g):
                        pe.wait_ge(p_made, NG * i + g + 1)
                        for half in range(2):
                            wait_turn(pe, "pt", 2 * g + half, i)
                            bank = turn_bank("pt", 2 * g + half)
                            for a in range(4):
                                h, slot = 2 * half + a // 2, a % 2
                                last = nc.tensor.transpose(bank[:, a * P:(a + 1) * P],
                                                           prob[:, g % 2, h, slot * P:(slot + 1) * P], ident[:, :])
                            last.then_inc(pt_done, 1)

                    scores(i, 1)
                    for ch in range(2):
                        if front:
                            pe.wait_ge(k_by, 2 * (i + 1) + ch + 1)
                        else:
                            pe.wait_ge(q_by, 2 * i + ch + 1)
                        project(s, ch, VC + ch * 512, vp_done)
                    if exists(j, s - 1):
                        pe.wait_ge(pt_low, 2 * NG * i)
                        pe.wait_ge(ctx_made, NG * i - 1)
                        values_product(NG - 1)
                    transpose_prob(0)
                    scores(i, 2)
                    if exists(j, s - 1):
                        pe.wait_ge(ctx_made, NG * i)
                        for b in range(2):
                            wait_turn(pe, "tc", b, i)
                            for a in range(4):
                                last = nc.tensor.transpose(turn_bank("tc", b)[:, a * P:(a + 1) * P],
                                                           ctx[:, (4 * b + a) * P:(4 * b + a + 1) * P], ident[:, :])
                            last.then_inc(tc_done, 1)
                    if front:
                        queries(1 - s, v_low, 2 * i)
                    pe.wait_ge(v_low, 2 * i + 2)
                    pe.wait_ge(pt_low, 2 * NG * i + 2)
                    values_product(0)
                    transpose_prob(1)
                    scores(i, 3)
                    if ahead:
                        wait_turn(pe, "tx", 0, i)
                        transpose_x(i + 2, turn_bank("tx", 0))
                    if front:
                        wait_turn(pe, "tk", 0, i)
                        transpose_rope(i + 1, 0, k_rope, k_roped, turn_bank("tk", 0), tk_done)
                        wait_turn(pe, "tq", 0, i)
                        transpose_rope(i + 1, 0, q_rope, q_roped, turn_bank("tq", 0), tq_done)
                    pe.wait_ge(ctx_made, NG * i + 1)
                    if exists(j, s - 1):
                        output(i - 1)
                    transpose_prob(2)
                    pe.wait_ge(pt_low, 2 * NG * i + 4)
                    if exists(j, s - 1):
                        pe.wait_ge(x_made, i)
                    values_product(1)
                    if front:
                        scores(i + 1, 0)
                        wait_turn(pe, "tk", 1, i)
                        transpose_rope(i + 1, 1, k_rope, k_roped, turn_bank("tk", 1), tk_done)
                        wait_turn(pe, "tq", 1, i)
                        transpose_rope(i + 1, 1, q_rope, q_roped, turn_bank("tq", 1), tq_done)
                    if ahead:
                        pe.wait_ge(xt_low, i + 3)
                        keys(i + 2, s)
                    pe.wait_ge(pt_low, 2 * NG * i + 6)
                    pe.wait_ge(ctx_made, NG * i + 2)
                    values_product(2)
                    transpose_prob(3)
            over_pairs(pair)(pe)
            pe.wait_ge(pt_low, 2 * NG * NBLK)
            pe.wait_ge(ctx_made, NG * NBLK - 1)
            values_product(NG - 1)
            pe.wait_ge(ctx_made, NG * NBLK)
            for b in range(2):
                wait_turn(pe, "tc", b, NBLK)
                for a in range(4):
                    last = nc.tensor.transpose(turn_bank("tc", b)[:, a * P:(a + 1) * P],
                                               ctx[:, (4 * b + a) * P:(4 * b + a + 1) * P], ident[:, :])
                last.then_inc(tc_done, 1)
            output(NBLK - 1)


def build(nc, x, wa_t, ba, wq_t, bq, wk_t, bk, wv, bv, wo_t, bo, wr_t, wkk_t, wvv_t, mu_r, mu_k, cos, sin, sin_neg,
          out):
    x1 = nc.dram_tensor("x_after_ffn", (P, NBLK, C), F32, kind="Internal").ap()
    x2 = nc.dram_tensor("x_after_attention", (P, NBLK, C), F32, kind="Internal").ap()
    with ExitStack() as sems:
        ffn_phase(nc, sems, "f1", x, x1, wr_t, wkk_t, wvv_t, mu_r, mu_k, value=(wa_t, ba))
        attention_phase(nc, sems, x1, x2, wq_t, wk_t, wv, wo_t, bq, bk, bv, bo, cos, sin, sin_neg)
        ffn_phase(nc, sems, "f2", x2, out, wr_t, wkk_t, wvv_t, mu_r, mu_k)


def rope_tables():
    freq = (1.0 / np.power(np.float32(10000.0), np.arange(0, HD, 2, dtype=np.float32) / np.float32(HD))).astype(np.float32)
    angle = np.arange(SEQ, dtype=np.float32)[:, None] * freq[None, :]
    lay = lambda a: np.ascontiguousarray(a.astype(np.float32).reshape(BPB, P, HD // 2).transpose(1, 0, 2))
    return lay(np.cos(angle)), lay(np.sin(angle)), lay(-np.sin(angle))


def kernel(**inputs):
    import numpy as _np
    import concourse.bacc as _bacc
    from concourse import mybir as _mybir
    from concourse.bass_utils import run_bass_kernel_spmd as _run

    lay = _np.ascontiguousarray
    a = {name: _np.asarray(value) for name, value in inputs.items()}
    cos, sin, sin_neg = rope_tables()
    arrays = {
        "x": lay(a["L0_attn_a_x"].reshape(NBLK, P, C).transpose(1, 0, 2)),
        "wa_t": lay(a["L0_attn_a_W"].T), "ba": lay(a["L0_attn_a_b"]),
        "wq_t": lay(a["L0_attn_b_Wq"].T), "bq": lay(a["L0_attn_b_bq"]),
        "wk_t": lay(a["L0_attn_b_Wk"].T), "bk": lay(a["L0_attn_b_bk"]),
        "wv": lay(a["L0_attn_b_Wv"]), "bv": lay(a["L0_attn_b_bv"].reshape(QKV // P, P).T),
        "wo_t": lay(a["L0_attn_b_Wo"].T), "bo": lay(a["L0_attn_b_bo"]),
        "wr_t": lay(a["L0_ffn_W_r"].T), "wkk_t": lay(a["L0_ffn_W_k"].T), "wvv_t": lay(a["L0_ffn_W_v"].T),
        "mu_r": lay(a["L0_ffn_mu_r"].reshape(CK, P).T), "mu_k": lay(a["L0_ffn_mu_k"].reshape(CK, P).T),
        "cos": cos, "sin": sin, "sin_neg": sin_neg,
    }
    nc = _bacc.Bacc("TRN2", target_bir_lowering=False, num_devices=1)
    args = [nc.dram_tensor(f"in_{n}", v.shape, _mybir.dt.from_np(v.dtype), kind="ExternalInput").ap()
            for n, v in arrays.items()]
    out = nc.dram_tensor("out_x", (P, NBLK, C), _mybir.dt.float32, kind="ExternalOutput").ap()
    build(nc, *args, out)
    r = _run(nc, [{f"in_{n}": v for n, v in arrays.items()}], core_ids=[0])
    got = r.results[0]["out_x"]
    return lay(got.transpose(1, 0, 2)).reshape(BATCH, SEQ, C)
```

```python
from contextlib import ExitStack

import concourse.bass as bass
import numpy as np
from concourse import mybir

F32 = mybir.dt.float32
F32R = mybir.dt.float32r
F16 = mybir.dt.float16
ALU = mybir.AluOpType
ACT = mybir.ActivationFunctionType
AX = mybir.AxisListType

P = 128
BATCH, SEQ, C = 4, 2048, 256
NBLK = BATCH * SEQ // P
BPB = SEQ // P
CK = C // P
EPS = 1e-5

HEADS, HD = 16, 64
QKV = HEADS * HD
GROUP = 4
NG = HEADS // GROUP
SCALE = 1.0 / float(np.sqrt(HD))
MASKED = -1e30
V_TOP = 2.0**14


class Need:

    def __init__(self, eng):
        self.eng = eng

    def __call__(self, sem, count):
        if not isinstance(count, int) or count > 0:
            self.eng.wait_ge(sem, count)


def identity(nc, pool, tile, made, n=1):
    nc.gpsimd.memset(tile[:, :], 0.0).then_inc(made, 1)
    pool.wait_ge(made, n)
    nc.gpsimd.affine_select(out=tile[:, :], in_=tile[:, :], compare_op=ALU.not_equal, fill=1.0,
                            base=0, pattern=[[-1, P]], channel_multiplier=1).then_inc(made, 1)


def ffn_constants(nc, stack):
    def sb(what, shape, dt=F32):
        return stack.enter_context(nc.sbuf_tensor(f"ffn_{what}", shape, dt))
    return (sb("w_h", [P, 3, CK, C], F32R), sb("w_l", [P, 3, CK, C], F32R), sb("mu", [P, 2, CK]), sb("ident", [P, P]))


def ffn_phase(nc, sems, name, x_in, x_out, tiles, weights=None, value=None):
    CB = 4
    N = CB * P
    CHUNKS = NBLK // CB
    CPB = CHUNKS // BATCH
    SLOTS = 4
    R, K = 0, 1
    HIGH, LOW = 0, 1
    TERMS = ((HIGH, HIGH), (LOW, HIGH), (HIGH, LOW))

    def sem(what):
        return sems.enter_context(nc.semaphore(f"{name}_{what}"))

    with ExitStack() as mem:
        def sb(what, shape, dt=F32):
            return mem.enter_context(nc.sbuf_tensor(f"{name}_{what}", shape, dt))

        def bank(what):
            return mem.enter_context(nc.psum_tensor(f"{name}_{what}", [P, 2, 512], F32))

        x_raw = sb("x_raw", [P, 2, CB, C])
        x = sb("x", [P, SLOTS, CB, C])
        x_new = sb("x_new", [P, 2, CB, C])
        xn = sb("xn", [P, CB, C])
        stats = sb("stats", [P, CB, 6])
        mv = sb("mv", [P, CB, 2])
        veps = sb("veps", [P, CB])
        rstd = sb("rstd", [P, CB])
        power = sb("power", [P, CB])
        eps = sb("eps", [P, CB])
        carrier = sb("carrier", [P, 1])
        xt = sb("xt", [P, 2, CK, N + 1])
        zero = sb("zero", [P, CK, 1])
        step = sb("step", [P, CK, N])
        mix = sb("mix", [P, 2, CK, N])
        mix_h = sb("mix_h", [P, 2, CK, N], F32R)
        mix_l = sb("mix_l", [P, 2, CK, N], F32R)
        relu = sb("relu", [P, CK, N])
        act = sb("act", [P, CK, N])
        act_h = sb("act_h", [P, CK, N], F32R)
        act_l = sb("act_l", [P, CK, N], F32R)
        gate = sb("gate", [P, 2, 2 * C])
        gated = sb("gated", [P, 2, 2 * C])
        if weights is not None:
            w_raw = sb("w_raw", [P, 3, CK, C])
        w_h, w_l, mu, ident = tiles
        WR, WK, WV = range(3)

        t_ps = bank("t_ps")
        k_ps = bank("k_ps")
        r_ps = bank("r_ps")
        v_ps = bank("v_ps")

        load = [sem(f"load{s}") for s in range(2)]
        stored = [sem(f"stored{s}") for s in range(2)]
        consts = sem("consts")
        ident_made = sem("ident_made")
        w_high = sem("w_high")
        w_low = sem("w_low")
        valued = sem("valued")
        stats_made = sem("stats_made")
        mv_made = sem("mv_made")
        veps_made = sem("veps_made")
        rstd_made = sem("rstd_made")
        xn_made = sem("xn_made")
        t_done = sem("t_done")
        xt_made = sem("xt_made")
        step_made = sem("step_made")
        mix_made = sem("mix_made")
        mixh_made = sem("mixh_made")
        mixl_made = sem("mixl_made")
        k_done = sem("k_done")
        relu_made = sem("relu_made")
        act_made = sem("act_made")
        acth_made = sem("acth_made")
        actl_made = sem("actl_made")
        r_done = sem("r_done")
        gate_made = sem("gate_made")
        v_done = sem("v_done")
        gated_made = sem("gated_made")
        x_made = sem("x_made")

        if value is not None:
            value_wt, value_b = value
            wa = sb("wa", [P, CK, C])
            ba = sb("ba", [P, C])
            vb = sb("vb", [P, BATCH, C])
            value_in = sem("value_in")
            wa_in = sem("wa_in")
            va_mv = sem("va_mv")
            va_rstd = sem("va_rstd")
            va_xn = sem("va_xn")
            va_t = sem("va_t")
            va_xt = sem("va_xt")
            va_done = sem("va_done")
            vb_made = sem("vb_made")
            value_now = sb("value_now", [P, C])
            value_now_made = sem("value_now_made")

        def chunk(ap, c):
            return ap[:, bass.ts(c, CB), :]

        block = mem.enter_context(nc.Block())

        def over_batches(body):
            def run(eng):
                body(eng, 0)
                with eng.Fori(1, BATCH - 1) as b:
                    body(eng, b)
                body(eng, BATCH - 1)
            return run

        def before(b, s):
            return not isinstance(b, int) or b * CPB + s > 0

        def remain(b, s, ahead):
            return not isinstance(b, int) or b * CPB + s + ahead < CHUNKS

        @block.sync
        def _(sp):
            need = Need(sp)
            if value is not None:
                for b in range(BATCH):
                    sp.dma_start(xn[:, b, :], x_in[1, b * BPB, :].partition_broadcast(P)).then_inc(value_in, 16)
            def fetch(c, s):
                sp.dma_start(x_raw[:, s % 2, :, :], chunk(x_in, c)).then_inc(load[s % 2], 16)

            for s in range(2):
                fetch(s, s)
            for s in range(2, 4):
                sp.wait_ge(valued, s - 1)
                fetch(s, s)

            def store(c, s):
                sp.dma_start(chunk(x_out, c), x_new[:, s % 2, :, :]).then_inc(stored[s % 2], 16)

            def batch(sp, b):
                for s in range(CPB):
                    c = b * CPB + s
                    if before(b, s):
                        sp.wait_ge(x_made, c)
                        store(c - 1, s + 1)
                    if remain(b, s, 4):
                        sp.wait_ge(valued, c + 3)
                        fetch(c + 4, s)
            over_batches(batch)(sp)
            sp.wait_ge(x_made, CHUNKS)
            store(CHUNKS - 1, 1)
            for s in range(2):
                sp.wait_ge(stored[s], 16 * CHUNKS // 2)

        @block.gpsimd
        def _(pool):
            need = Need(pool)
            nc.gpsimd.memset(power[:, :], -0.5).then_inc(ident_made, 1)
            nc.gpsimd.memset(eps[:, :], EPS)
            nc.gpsimd.memset(zero[:, :, :], 0.0).then_inc(ident_made, 1)
            if weights is not None:
                identity(nc, pool, ident, ident_made, 3)
            pool.wait_ge(ident_made, 2)

            def inverse_std(n, made):
                nc.gpsimd.tensor_tensor(veps[:, :], mv[:, :, 1], eps[:, :], ALU.add).then_inc(veps_made, 1)
                pool.wait_ge(veps_made, n)
                nc.gpsimd.tensor_tensor(rstd[:, :], veps[:, :], power[:, :], ALU.pow).then_inc(made, 1)

            first = 1 if value is not None else 0
            if value is not None:
                pool.wait_ge(va_mv, 1)
                inverse_std(1, va_rstd)

            def next_value(b):
                if value is not None:
                    nc.gpsimd.tensor_copy(value_now[:, :], vb[:, b, :]).then_inc(value_now_made, 1)

            def take(b, slot, loads):
                if value is None:
                    return
                pool.wait_ge(load[slot % 2], 16 * loads)
                pool.wait_ge(value_now_made, b + 1)
                row = value_now[:, :].unsqueeze(1).broadcast_to([P, CB, C])
                nc.gpsimd.tensor_tensor(x[:, slot, :, :], x_raw[:, slot % 2, :, :], row,
                                        ALU.add).then_inc(valued, 1)

            def std_of(c):
                pool.wait_ge(mv_made, c + 1)
                need(xn_made, c)
                inverse_std(c + 1 + first, rstd_made)

            def step_of(c, s):
                pool.wait_ge(xt_made, c + 1)
                need(mix_made, 2 * c)
                for k in range(CK):
                    nc.gpsimd.tensor_tensor(step[:, k, :], xt[:, s % 2, k, 1:N + 1], xt[:, s % 2, k, 0:N],
                                            ALU.subtract).then_inc(step_made, 1)

            if value is not None:
                pool.wait_ge(vb_made, 1)
            next_value(0)
            take(0, 0, 1)
            std_of(0)
            take(0, 1, 1)
            step_of(0, 0)
            std_of(1)
            take(0, 2, 2)

            def add_gated(c, s):
                need(stored[s % 2], 16 * (c // 2) if isinstance(c, int) else 8 * (c - s % 2))
                for h in range(2):
                    pool.wait_ge(gated_made, 2 * c + h + 1)
                    flat = lambda tile: tile.rearrange("p (h a) c -> p h (a c)", h=2)[:, h]
                    last = nc.gpsimd.tensor_tensor(flat(x_new[:, s % 2, :, :]), flat(x[:, s % SLOTS, :, :]),
                                                   gated[:, h, :], ALU.add)
                last.then_inc(x_made, 1)

            def batch(pool, b):
                for s in range(CPB):
                    c = b * CPB + s
                    if remain(b, s, 1):
                        step_of(c + 1, s + 1)
                    if remain(b, s, 2):
                        std_of(c + 2)
                    if remain(b, s, 3) and s == 1 and value is not None:
                        pool.wait_ge(valued, CPB * (b + 1))
                    if before(b, s):
                        add_gated(c - 1, (s + SLOTS - 1) % SLOTS)
                    if remain(b, s, 3):
                        ahead = b + (s + 3) // CPB
                        if s == 1 and value is not None:
                            next_value(ahead)
                        if value is not None:
                            need(x_made, c)
                        take(ahead, (s + 3) % SLOTS, 2 * ahead + (s + 3) % CPB // 2 + 1)
            over_batches(batch)(pool)
            add_gated(CHUNKS - 1, SLOTS - 1)

        @block.vector
        def _(dve):
            need = Need(dve)
            def moments(src, n, made):
                for j in range(CB):
                    last = nc.vector.bn_stats(stats[:, j, :], src[:, j, :])
                last.then_inc(stats_made, 1)
                dve.wait_ge(stats_made, n)
                nc.vector.memset(carrier[:, :], 0.0)
                for j in range(CB):
                    last = nc.vector.bn_aggr(mv[:, j, :], stats[:, j, :])
                last.then_inc(made, 1)

            def normalize(src, made):
                for j in range(CB):
                    last = nc.vector.tensor_scalar(xn[:, j, :], src[:, j, :], mv[:, j, 0:1], rstd[:, j:j + 1],
                                                   ALU.subtract, ALU.mult)
                last.then_inc(made, 1)

            first = 1 if value is not None else 0
            if value is not None:
                dve.wait_ge(value_in, 16 * BATCH)
                moments(xn, 1, va_mv)
                dve.wait_ge(va_rstd, 1)
                normalize(xn, va_xn)
            if weights is not None:
                dve.wait_ge(consts, 16 * 5)
                dve.wait_ge(w_high, 1)
                nc.vector.tensor_tensor(w_l[:, :, :, :], w_raw[:, :, :, :], w_h[:, :, :, :].bitcast(F32),
                                        ALU.subtract).then_inc(w_low, 1)
            if value is not None:
                for b in range(BATCH):
                    dve.wait_ge(va_done, b + 1)
                    nc.vector.tensor_tensor(vb[:, b, :], (k_ps, v_ps)[b // 2][:, b % 2, 0:C],
                                            ba[:, :], ALU.add).then_inc(vb_made, 1)

            def moments_of(c, slot):
                dve.wait_ge(valued, c + 1)
                need(rstd_made, c)
                need(xn_made, c)
                moments(x[:, slot, :, :], c + 1 + first, mv_made)

            def normalize_of(c, slot):
                dve.wait_ge(rstd_made, c + 1)
                need(t_done, c)
                if value is not None:
                    dve.wait_ge(va_t, BATCH)
                normalize(x[:, slot, :, :], xn_made)

            def mix_of(c, s):
                need(mixh_made, 2 * c)
                need(mixl_made, 2 * c)
                for k in range(CK):
                    dve.wait_ge(step_made, CK * c + k + 1)
                    for m in (K, R):
                        last = nc.vector.scalar_tensor_tensor(
                            mix[:, m, k, :], step[:, k, :], mu[:, m, k:k + 1], xt[:, s % 2, k, 0:N],
                            ALU.mult, ALU.add)
                        if k == CK - 1:
                            last.then_inc(mix_made, 1)

            def mix_low(c, n):
                m = (K, R)[n]
                dve.wait_ge(mixh_made, 2 * c + n + 1)
                need((k_done, r_done)[n], 2 * c)
                nc.vector.tensor_tensor(mix_l[:, m, :, :], mix[:, m, :, :], mix_h[:, m, :, :].bitcast(F32),
                                        ALU.subtract).then_inc(mixl_made, 1)

            moments_of(0, 0)
            normalize_of(0, 0)
            moments_of(1, 1)
            mix_of(0, 0)
            normalize_of(1, 1)
            mix_low(0, 0)
            mix_low(0, 1)

            def act_low(c):
                for m in range(CK):
                    dve.wait_ge(acth_made, CK * c + m + 1)
                    need(v_done, 2 * c)
                    nc.vector.tensor_tensor(act_l[:, m, :], act[:, m, :], act_h[:, m, :].bitcast(F32),
                                            ALU.subtract).then_inc(actl_made, 1)

            def gate_value(c):
                need(x_made, c)
                for h in range(2):
                    dve.wait_ge(gate_made, 2 * c + h + 1)
                    dve.wait_ge(v_done, 2 * c + h + 1)
                    nc.vector.tensor_tensor(gated[:, h, :], v_ps[:, h, :], gate[:, h, :],
                                            ALU.mult).then_inc(gated_made, 1)

            def batch(dve, b):
                for s in range(CPB):
                    c = b * CPB + s
                    if remain(b, s, 2):
                        moments_of(c + 2, (s + 2) % SLOTS)
                    if remain(b, s, 1):
                        mix_of(c + 1, s + 1)
                    if before(b, s):
                        gate_value(c - 1)
                    if remain(b, s, 1):
                        mix_low(c + 1, 0)
                    if remain(b, s, 2):
                        normalize_of(c + 2, (s + 2) % SLOTS)
                    act_low(c)
                    if remain(b, s, 1):
                        mix_low(c + 1, 1)
            over_batches(batch)(dve)
            gate_value(CHUNKS - 1)

        @block.scalar
        def _(act_e):
            need = Need(act_e)
            if value is not None:
                act_e.dma_start(wa[:, :, :], value_wt.rearrange("(k p) c -> p k c", p=P)).then_inc(wa_in, 16)
                act_e.dma_start(ba[:, :], value_b.partition_broadcast(P)).then_inc(wa_in, 16)
            if weights is not None:
                wr_t, wk_t, wv_t, mu_r, mu_k = weights
                for w, ap in ((WR, wr_t), (WK, wk_t), (WV, wv_t)):
                    act_e.dma_start(w_raw[:, w, :, :], ap.rearrange("(k p) c -> p k c", p=P)).then_inc(consts, 16)
                act_e.dma_start(mu[:, R, :], mu_r).then_inc(consts, 16)
                act_e.dma_start(mu[:, K, :], mu_k).then_inc(consts, 16)
                act_e.wait_ge(consts, 16 * 5)
                nc.scalar.activation(w_h[:, :, :, :], w_raw[:, :, :, :], ACT.Copy).then_inc(w_high, 1)
            if value is not None:
                act_e.wait_ge(va_t, BATCH)
                for b in range(BATCH):
                    nc.scalar.activation(mix[:, b // 2, :, (b % 2) * P:(b % 2 + 1) * P],
                                         t_ps[:, :, b * P:(b + 1) * P], ACT.Copy).then_inc(va_xt, 1)

            def transposed(c, s):
                act_e.wait_ge(t_done, c + 1)
                need(mix_made, 2 * (c - 1))
                if s % CPB == 0:
                    before = zero[:, :, :]
                    act_e.wait_ge(ident_made, 2)
                else:
                    before = xt[:, (s - 1) % 2, :, N:N + 1]
                    need(xt_made, c)
                nc.scalar.activation(xt[:, s % 2, :, 0:1], before, ACT.Copy)
                nc.scalar.activation(xt[:, s % 2, :, 1:N + 1], t_ps[:, :, :], ACT.Copy).then_inc(xt_made, 1)

            def mix_high(c, n):
                m = (K, R)[n]
                act_e.wait_ge(mix_made, 2 * c + n + 1)
                need((k_done, r_done)[n], 2 * c)
                nc.scalar.activation(mix_h[:, m, :, :], mix[:, m, :, :], ACT.Copy).then_inc(mixh_made, 1)

            def act_high(c, m):
                act_e.wait_ge(act_made, CK * c + m + 1)
                need(v_done, 2 * c)
                nc.scalar.activation(act_h[:, m, :], act[:, m, :], ACT.Copy).then_inc(acth_made, 1)

            def take(slot, loads):
                act_e.wait_ge(load[slot % 2], 16 * loads)
                nc.scalar.activation(x[:, slot, :, :], x_raw[:, slot % 2, :, :], ACT.Copy).then_inc(valued, 1)

            if value is None:
                for s in range(2):
                    take(s, 1)
                take(2, 2)
            transposed(0, 0)
            mix_high(0, 0)
            mix_high(0, 1)

            def batch(act_e, b):
                for s in range(CPB):
                    c = b * CPB + s
                    if remain(b, s, 1):
                        transposed(c + 1, s + 1)
                    for m in range(CK):
                        act_e.wait_ge(k_done, CK * c + m + 1)
                        need(act_made, CK * (c - 1) + m + 1)
                        nc.scalar.activation(relu[:, m, :], k_ps[:, m, :], ACT.Relu).then_inc(relu_made, 1)
                    for m in range(CK):
                        act_e.wait_ge(relu_made, CK * c + m + 1)
                        need(acth_made, CK * (c - 1) + m + 1)
                        need(actl_made, CK * (c - 1) + m + 1)
                        nc.scalar.activation(act[:, m, :], relu[:, m, :], ACT.Square).then_inc(act_made, 1)
                    if remain(b, s, 1):
                        mix_high(c + 1, 0)
                    for m in range(CK):
                        act_high(c, m)
                    if remain(b, s, 1):
                        mix_high(c + 1, 1)
                    for h in range(2):
                        act_e.wait_ge(r_done, 2 * c + h + 1)
                        need(gated_made, 2 * (c - 1) + h + 1)
                        nc.scalar.activation(gate[:, h, :], r_ps[:, h, :], ACT.Sigmoid).then_inc(gate_made, 1)
                    if value is None and remain(b, s, 3):
                        ahead = b + (s + 3) // CPB
                        need(x_made, c)
                        take((s + 3) % SLOTS, 2 * ahead + (s + 3) % CPB // 2 + 1)
            over_batches(batch)(act_e)

        @block.tensor
        def _(pe):
            need = Need(pe)
            w_parts = (w_h, w_l)
            if weights is not None:
                pe.wait_ge(ident_made, 4)
            if value is not None:
                pe.wait_ge(va_xn, 1)
                for b in range(BATCH):
                    for k in range(CK):
                        last = nc.tensor.transpose(t_ps[:, k, b * P:(b + 1) * P],
                                                   xn[:, b, k * P:(k + 1) * P], ident[:, :])
                    last.then_inc(va_t, 1)
                pe.wait_ge(va_xt, BATCH)
                pe.wait_ge(wa_in, 32)
                for b in range(BATCH):
                    for k in range(CK):
                        last = nc.tensor.matmul((k_ps, v_ps)[b // 2][:, b % 2, 0:C],
                                                mix[:, b // 2, k, (b % 2) * P:(b % 2 + 1) * P], wa[:, k, :],
                                                start=k == 0, stop=k == CK - 1)
                    last.then_inc(va_done, 1)

            def transposes(c):
                pe.wait_ge(xn_made, c + 1)
                need(xt_made, c)
                for k in range(CK):
                    for j in range(CB):
                        last = nc.tensor.transpose(t_ps[:, k, j * P:(j + 1) * P],
                                                   xn[:, j, k * P:(k + 1) * P], ident[:, :])
                last.then_inc(t_done, 1)

            transposes(0)
            if weights is not None:
                pe.wait_ge(w_low, 1)

            def values(c):
                pe.wait_ge(actl_made, CK * (c + 1))
                for h in range(2):
                    need(gated_made, 2 * (c - 1) + h + 1)
                    if value is not None and isinstance(c, int) and c == 0:
                        pe.wait_ge(vb_made, BATCH)
                    for j in range(2):
                        t = (2 * h + j) * P
                        for n, (wp, xp) in enumerate(TERMS):
                            for k in range(CK):
                                last = nc.tensor.matmul(
                                    v_ps[:, h, j * C:(j + 1) * C],
                                    (act_h, act_l)[xp][:, k, t:t + P], w_parts[wp][:, WV, k, :],
                                    start=n == 0 and k == 0, stop=n == 2 and k == CK - 1)
                    last.then_inc(v_done, 1)

            def batch(pe, b):
                for s in range(CPB):
                    c = b * CPB + s
                    if remain(b, s, 1):
                        transposes(c + 1)
                    pe.wait_ge(mixl_made, 2 * c + 1)
                    for m in range(CK):
                        need(relu_made, CK * (c - 1) + m + 1)
                        for n, (wp, xp) in enumerate(TERMS):
                            for k in range(CK):
                                last = nc.tensor.matmul(
                                    k_ps[:, m, :], w_parts[wp][:, WK, k, m * P:(m + 1) * P],
                                    (mix_h, mix_l)[xp][:, K, k, :],
                                    start=n == 0 and k == 0, stop=n == 2 and k == CK - 1)
                        last.then_inc(k_done, 1)
                    if before(b, s):
                        values(c - 1)
                    pe.wait_ge(mixl_made, 2 * c + 2)
                    for h in range(2):
                        need(gate_made, 2 * (c - 1) + h + 1)
                        for j in range(2):
                            t = (2 * h + j) * P
                            for n, (wp, xp) in enumerate(TERMS):
                                for k in range(CK):
                                    last = nc.tensor.matmul(
                                        r_ps[:, h, j * C:(j + 1) * C],
                                        (mix_h, mix_l)[xp][:, R, k, t:t + P], w_parts[wp][:, WR, k, :],
                                        start=n == 0 and k == 0, stop=n == 2 and k == CK - 1)
                        last.then_inc(r_done, 1)
            over_batches(batch)(pe)
            values(CHUNKS - 1)


def attention_phase(nc, sems, x_in, x_out, wq_t, wk_t, wv, wo_t, bq, bk, bv, bo, cos, sin, sin_neg):
    AHEAD = 2
    WCOLS = 8
    VE = HD + 1
    HI, LO = 0, 1
    TERMS = ((HI, HI), (HI, LO), (LO, HI))
    QC, KC, VC = 0, QKV, 2 * QKV

    def sem(what):
        return sems.enter_context(nc.semaphore(f"at_{what}"))

    with ExitStack() as mem:
        def sb(what, shape, dt=F32):
            return mem.enter_context(nc.sbuf_tensor(f"at_{what}", shape, dt))

        def pb(what, shape):
            return mem.enter_context(nc.psum_tensor(f"at_{what}", shape, F32))

        w_h = sb("w_h", [P, CK, 3 * QKV], F32R)
        w_l = sb("w_l", [P, CK, 3 * QKV], F32R)
        wo_h = sb("wo_h", [P, WCOLS, C], F32R)
        wo_l = sb("wo_l", [P, WCOLS, C], F32R)
        raw = sb("raw", [P, 2, CK * QKV])
        cos_sb = sb("cos", [P, BPB, HD // 2])
        sin_sb = sb("sin", [P, BPB, HD // 2])
        nsin_sb = sb("nsin", [P, BPB, HD // 2])
        bias = sb("bias", [P, 2 * QKV])
        bv_cols = sb("bv_cols", [P, WCOLS])
        out_bias = sb("out_bias", [P, C])
        wsum = sb("wsum", [P, WCOLS])
        v_down = sb("v_down", [P, WCOLS])
        v_up = sb("v_up", [P, WCOLS])
        masks = sb("masks", [P, 3, 2 * P])
        mask_even = sb("mask_even", [P, 2 * P])
        ident = sb("ident", [P, P])

        x_ln = sb("x_ln", [P, 2, C])
        x_res = sb("x_res", [P, 2, C])
        stats = sb("stats", [P, 6])
        mv = sb("mv", [P, 2])
        veps = sb("veps", [P, 1])
        power = sb("power", [P, 1])
        eps = sb("eps", [P, 1])
        carrier = sb("carrier", [P, 2])
        pool_carrier = sb("pool_carrier", [P, 1])
        rstd = sb("rstd", [P, 1])
        xn = sb("xn", [P, C])
        xt_h = sb("xt_h", [P, 2, CK, P], F32R)
        xt_l = sb("xt_l", [P, 2, CK, P], F32R)
        proj = sb("proj", [P, 2, 512])
        by_cos = sb("by_cos", [P, 2, 512])
        by_sin = sb("by_sin", [P, 2, 512])
        k_rope = sb("k_rope", [P, 2, 512])
        q_rope = sb("q_rope", [P, 2, 512])
        qt_h = sb("qt_h", [P, WCOLS, P], F32R)
        qt_l = sb("qt_l", [P, WCOLS, P], F32R)
        kt_h = sb("kt_h", [P, WCOLS, 2, P], F32R)
        kt_l = sb("kt_l", [P, WCOLS, 2, P], F32R)
        v_h = sb("v_h", [P, 2, HEADS, VE], F16)
        v_l = sb("v_l", [P, 2, HEADS, HD], F16)
        masked = sb("masked", [P, 2, GROUP, 2 * P])
        top = sb("top", [P, 2, GROUP])
        shift = sb("shift", [P, 2, GROUP])
        prob = sb("prob", [P, 2, GROUP, 2 * P])
        bv_wide = prob[:, 0, :, :].rearrange("p a (b c) -> p (a b) c", b=2)
        pt_h = sb("pt_h", [P, 2, 2, 512], F16)
        pt_l = sb("pt_l", [P, 2, 2, 512], F16)
        inv = sb("inv", [P, GROUP, 1])
        ctx = raw[:, 1, 0:QKV]
        ct_h = sb("ct_h", [P, WCOLS, P], F32R)
        ct_l = sb("ct_l", [P, WCOLS, P], F32R)

        s_ps = pb("s_ps", [P, 2, 512])
        pr_ps = pb("pr_ps", [P, 2, 512])
        c_ps = pb("c_ps", [P, 512])
        tb = [pb(f"tb{n}", [P, 512]) for n in range(3)]

        tab_in = sem("tab_in")
        raw_in = [sem("raw_in0"), sem("raw_in1")]
        made = sem("made")
        w_high = sem("w_high")
        w_low = sem("w_low")
        w_free = sem("w_free")
        v_chain = sem("v_chain")
        v_scaled = sem("v_scaled")
        wo_scaled = sem("wo_scaled")
        bv_made = sem("bv_made")
        ob_done = sem("ob_done")
        out_bias_made = sem("out_bias_made")
        res_biased = sem("res_biased")
        wt_done = sem("wt_done")
        wt_high = sem("wt_high")
        wt_low = sem("wt_low")

        ln_in = [sem("ln_in0"), sem("ln_in1")]
        res_in = [sem("res_in0"), sem("res_in1")]
        stored = [sem("stored0"), sem("stored1")]
        stats_made = sem("stats_made")
        mv_made = sem("mv_made")
        veps_made = sem("veps_made")
        rstd_made = sem("rstd_made")
        xn_made = sem("xn_made")
        tx_done = sem("tx_done")
        xt_high = sem("xt_high")
        xt_low = sem("xt_low")
        k_done = sem("k_done")
        q_done = sem("q_done")
        k_copied = sem("k_copied")
        k_biased = sem("k_biased")
        q_biased = sem("q_biased")
        cos_made = sem("cos_made")
        k_by = sem("k_by")
        q_by = sem("q_by")
        k_roped = sem("k_roped")
        q_roped = sem("q_roped")
        tk_done = sem("tk_done")
        tq_done = sem("tq_done")
        kt_high = sem("kt_high")
        kt_low = sem("kt_low")
        qt_high = sem("qt_high")
        qt_low = sem("qt_low")
        vp_done = sem("vp_done")
        v_high = sem("v_high")
        v_low = sem("v_low")
        s_done = sem("s_done")
        top_made = sem("top_made")
        shift_made = sem("shift_made")
        p_made = sem("p_made")
        pt_done = sem("pt_done")
        pt_high = sem("pt_high")
        pt_low = sem("pt_low")
        pv_done = sem("pv_done")
        inv_made = sem("inv_made")
        ctx_made = sem("ctx_made")
        tc_done = sem("tc_done")
        ct_high = sem("ct_high")
        ct_low = sem("ct_low")
        wo_done = sem("wo_done")
        x_made = sem("x_made")
        mask_made = sem("mask_made")

        TURNS = [("pt", 0), ("pt", 1), ("tc", 0), ("tc", 1), ("pt", 2), ("pt", 3), ("tx", 0), ("tk", 0),
                 ("tq", 0), ("pt", 4), ("pt", 5), ("tk", 1), ("tq", 1), ("pt", 6), ("pt", 7)]
        LOW = {"pt": pt_low, "tc": ct_low, "tk": kt_low, "tq": qt_low, "tx": xt_low}

        def present(what, i):
            if not isinstance(i, int):
                return True
            return {"pt": 0 <= i < NBLK, "tc": i >= 1, "tk": 0 <= i < NBLK - 1, "tq": 0 <= i < NBLK - 1,
                    "tx": 0 <= i < NBLK - AHEAD}[what]

        def low_count(what, i, n):
            return {"pt": 2 * NG * i + n + 1, "tc": 2 * (i - 1) + n + 1, "tk": 2 * (i + 1) + n + 1,
                    "tq": 2 * (i + 1) + n + 1, "tx": i + AHEAD + 1}[what]

        def turn_bank(what, n):
            return tb[TURNS.index((what, n)) % 3]

        def wait_turn(pe, what, n, i):
            at = TURNS.index((what, n)) - 3
            step = i
            while True:
                if at < 0:
                    at, step = at + len(TURNS), step - 1
                if isinstance(step, int) and step < 0:
                    pe.wait_ge(qt_low, 2)
                    pe.wait_ge(xt_low, AHEAD)
                    return
                if present(TURNS[at][0], step):
                    pe.wait_ge(LOW[TURNS[at][0]], low_count(TURNS[at][0], step, TURNS[at][1]))
                    return
                at -= 3

        def count(j, q, per=1):
            return 16 * per * (j + q // 2 + 1)

        MADE = 3 + 6 + 5 + 1
        block = mem.enter_context(nc.Block())

        def over_pairs(body):
            def run(eng):
                body(eng, 0)
                with eng.Fori(1, NBLK // 2 - 1) as j:
                    body(eng, j)
                body(eng, NBLK // 2 - 1)
            return run

        def exists(j, q):
            return not isinstance(j, int) or 0 <= 2 * j + q < NBLK

        @block.sync
        def _(sp):
            need = Need(sp)
            for s in range(AHEAD):
                sp.dma_start(x_ln[:, s, :], x_in[:, s, :]).then_inc(ln_in[s], 16)

            def weights(n, ap):
                need(w_free, n - 1)
                sp.dma_start(raw[:, n % 2, :].rearrange("p (a b) -> p a b", a=ap.shape[0] // P),
                             ap.rearrange("(k p) c -> p k c", p=P)).then_inc(raw_in[n % 2], 16)
            weights(0, wk_t)
            weights(1, wq_t)
            tables = [(cos_sb[:, :, :], cos), (sin_sb[:, :, :], sin), (nsin_sb[:, :, :], sin_neg),
                      (bv_cols[:, :], bv), (out_bias[:, :], bo.partition_broadcast(P)),
                      (bias[:, 0:QKV], bq.partition_broadcast(P)), (bias[:, QKV:], bk.partition_broadcast(P))]
            for dst, src in tables:
                sp.dma_start(dst, src).then_inc(tab_in, 16)
            weights(2, wv)
            weights(3, wo_t)

            def pair(sp, j):
                for s in range(2):
                    i = 2 * j + s
                    if exists(j, s + AHEAD):
                        sp.wait_ge(xn_made, i + 1)
                        sp.dma_start(x_ln[:, s, :], x_in[:, i + AHEAD, :]).then_inc(ln_in[s], 16)
                    need(stored[s], count(j, s) - 16)
                    sp.dma_start(x_res[:, s, :], x_in[:, i, :]).then_inc(res_in[s], 16)
                    if exists(j, s - 1):
                        sp.wait_ge(x_made, i)
                        sp.dma_start(x_out[:, i - 1, :], x_res[:, 1 - s, :]).then_inc(stored[1 - s], 16)
            over_pairs(pair)(sp)
            sp.wait_ge(x_made, NBLK)
            sp.dma_start(x_out[:, NBLK - 1, :], x_res[:, 1, :]).then_inc(stored[1], 16)
            for s in range(2):
                sp.wait_ge(stored[s], 16 * NBLK // 2)

        @block.gpsimd
        def _(pool):
            need = Need(pool)
            def inverse_std(t):
                pool.wait_ge(mv_made, t + 1)
                need(xn_made, t)
                nc.gpsimd.tensor_tensor(veps[:, :], mv[:, 1:2], eps[:, :], ALU.add).then_inc(veps_made, 1)
                pool.wait_ge(veps_made, t + 1)
                nc.gpsimd.tensor_tensor(rstd[:, :], veps[:, :], power[:, :], ALU.pow).then_inc(rstd_made, 1)

            nc.gpsimd.memset(power[:, :], -0.5)
            nc.gpsimd.memset(eps[:, :], EPS)
            nc.gpsimd.memset(masks[:, :, :], 0.0).then_inc(made, 1)
            identity(nc, pool, ident, made, 2)
            inverse_std(0)
            past = dict(compare_op=ALU.is_ge, fill=MASKED, base=0, pattern=[[1, P]], channel_multiplier=-1)
            own = dict(compare_op=ALU.is_ge, fill=MASKED, base=0, pattern=[[-1, P]], channel_multiplier=1)
            nc.gpsimd.memset(masks[:, 0, P:2 * P], MASKED).then_inc(made, 1)
            for m, half, kind in ((0, 0, own), (1, 0, own), (1, 1, past), (2, 0, past), (2, 1, own)):
                part = masks[:, m, half * P:(half + 1) * P]
                nc.gpsimd.affine_select(out=part, in_=part, **kind).then_inc(made, 1)
            nc.gpsimd.memset(kt_h[:, :, 1, :].bitcast(F32), 0.0).then_inc(made, 1)
            nc.gpsimd.memset(kt_l[:, :, 1, :].bitcast(F32), 0.0).then_inc(made, 1)
            nc.gpsimd.memset(v_h[:, 1, :, 0:HD], 0.0).then_inc(made, 1)
            nc.gpsimd.memset(v_h[:, :, :, HD:VE], 1.0).then_inc(made, 1)
            nc.gpsimd.memset(v_l[:, 1, :, :], 0.0).then_inc(made, 1)
            pool.wait_ge(made, MADE - 1)
            nc.gpsimd.tensor_copy(mask_even[:, :], masks[:, 0, :]).then_inc(made, 1)

            def rope(f, ch, n, kind):
                biased_by, by, rope_sb, roped, transposed = kind
                is_q = int(rope_sb is q_rope)
                nth = 4 * f + 2 * is_q + ch + 1
                if not is_q:
                    pool.wait_ge(k_copied, 2 * f + ch + 1)
                    nc.gpsimd.tensor_tensor(proj[:, ch, :], proj[:, ch, :],
                                            bias[:, QKV + ch * 512:QKV + ch * 512 + 512], ALU.add).then_inc(k_biased, 1)
                pool.wait_ge(biased_by, 2 * f + ch + 1)
                nc.gpsimd.tensor_tensor(pool_carrier[:, :], eps[:, :], eps[:, :], ALU.add)
                part = lambda tile: tile[:, ch, :].rearrange("p (h d) -> p h d", d=HD // 2)
                nc.gpsimd.tensor_tensor(part(by_cos), part(proj), cos_sb[:, n, :].unsqueeze(1).broadcast_to(
                    [P, 16, HD // 2]), ALU.mult).then_inc(cos_made, 1)
                pool.wait_ge(cos_made, nth)
                pool.wait_ge(by, 2 * f + ch + 1)
                need(transposed, 2 * (f - 1) + ch + 1)
                nc.gpsimd.tensor_tensor(rope_sb[:, ch, :], by_cos[:, ch, :], by_sin[:, ch, :],
                                        ALU.add).then_inc(roped, 1)

            keys = (k_biased, k_by, k_rope, k_roped, tk_done)
            queries = (q_biased, q_by, q_rope, q_roped, tq_done)
            inverse_std(1)
            pool.wait_ge(tab_in, 16 * 7)
            for ch in range(2):
                rope(0, ch, 0, keys)
            for ch in range(2):
                rope(0, ch, 0, queries)
            for ch in range(2):
                rope(1, ch, 1, keys)

            def pair(pool, j):
                for s in range(2):
                    i = 2 * j + s
                    if exists(j, s + 2):
                        inverse_std(i + 2)
                    pool.wait_ge(res_in[s], count(j, s))
                    pool.wait_ge(out_bias_made, 1)
                    nc.gpsimd.tensor_tensor(x_res[:, s, :], x_res[:, s, :], out_bias[:, :],
                                            ALU.add).then_inc(res_biased, 1)
                    if exists(j, s + 1):
                        for ch in range(2):
                            rope(i + 1, ch, (i + 1) % BPB, queries)
                    if exists(j, s + 2):
                        for ch in range(2):
                            rope(i + 2, ch, (i + 2) % BPB, keys)
            over_pairs(pair)(pool)

        @block.vector
        def _(dve):
            need = Need(dve)

            def moments(t, slot, loaded):
                dve.wait_ge(ln_in[slot], loaded)
                nc.vector.bn_stats(stats[:, :], x_ln[:, slot, :]).then_inc(stats_made, 1)
                dve.wait_ge(stats_made, t + 1)
                need(rstd_made, t)
                nc.vector.memset(carrier[:, 0:1], 0.0)
                nc.vector.bn_aggr(mv[:, :], stats[:, :]).then_inc(mv_made, 1)

            def normalize(t, slot):
                dve.wait_ge(rstd_made, t + 1)
                need(tx_done, t)
                nc.vector.tensor_scalar(xn[:, :], x_ln[:, slot, :], mv[:, 0:1], rstd[:, :],
                                        ALU.subtract, ALU.mult).then_inc(xn_made, 1)

            def low(out, src, high, sem_, dt=F32):
                high = high.bitcast(F32) if dt is F32 else high
                nc.vector.tensor_tensor(out, src, high, ALU.subtract).then_inc(sem_, 1)

            def xt_low_of(t, slot, bank):
                dve.wait_ge(xt_high, t + 1)
                low(xt_l[:, slot, :, :], bank[:, 0:C].rearrange("p (k t) -> p k t", k=CK),
                    xt_h[:, slot, :, :], xt_low)

            def sines(f, ch, n, biased, by):
                dve.wait_ge(biased, 2 * f + ch + 1)
                halves = proj[:, ch, :].rearrange("p (h e d) -> p e h d", e=2, d=HD // 2)
                out = by_sin[:, ch, :].rearrange("p (h e d) -> p e h d", e=2, d=HD // 2)
                for e, table in enumerate((nsin_sb, sin_sb)):
                    t = table[:, n, :].unsqueeze(1).broadcast_to([P, 8, HD // 2])
                    last = nc.vector.tensor_tensor(out[:, e], halves[:, 1 - e], t, ALU.mult)
                last.then_inc(by, 1)

            def key_sines(f, ch, n):
                sines(f, ch, n, k_biased, k_by)

            def query_sines(f, ch, n):
                sines(f, ch, n, q_biased, q_by)

            def query_bias(f, ch):
                if isinstance(f, int) and f == 0:
                    dve.wait_ge(tab_in, 16 * 7)
                dve.wait_ge(q_done, 2 * f + ch + 1)
                dve.wait_ge(k_roped, 2 * f + ch + 1)
                nc.vector.tensor_tensor(proj[:, ch, :], pr_ps[:, ch, :], bias[:, ch * 512:ch * 512 + 512],
                                        ALU.add).then_inc(q_biased, 1)

            def kt_low_of(f, b, slot, bank):
                dve.wait_ge(kt_high, 2 * f + b + 1)
                low(kt_l[:, 4 * b:4 * b + 4, slot, :], bank[:, :].rearrange("p (k t) -> p k t", k=4),
                    kt_h[:, 4 * b:4 * b + 4, slot, :], kt_low)

            def qt_low_of(f, b, bank):
                dve.wait_ge(qt_high, 2 * f + b + 1)
                low(qt_l[:, 4 * b:4 * b + 4, :], bank[:, :].rearrange("p (k t) -> p k t", k=4),
                    qt_h[:, 4 * b:4 * b + 4, :], qt_low)

            def weights_low(n, col):
                dve.wait_ge(w_high, n + 1)
                for k in range(CK):
                    last = nc.vector.tensor_tensor(
                        w_l[:, k, col:col + QKV], raw[:, n, k * QKV:(k + 1) * QKV],
                        w_h[:, k, col:col + QKV].bitcast(F32), ALU.subtract)
                last.then_inc(w_free, 1)

            def wv_low(n):
                dve.wait_ge(wt_high, n + 1)
                k, half = divmod(n, 2)
                cols = VC + half * 512
                nc.vector.tensor_tensor(w_l[:, k, cols:cols + 512], (s_ps[:, 0, :], s_ps[:, 1, :])[n % 2],
                                        w_h[:, k, cols:cols + 512].bitcast(F32), ALU.subtract).then_inc(wt_low, 1)

            moments(0, 0, 16)
            normalize(0, 0)
            moments(1, 1, 16)
            weights_low(0, KC)
            xt_low_of(0, 0, tb[0])
            normalize(1, 1)
            weights_low(1, QC)
            xt_low_of(1, 1, tb[1])
            key_sines(0, 0, 0)
            dve.wait_ge(raw_in[0], 32)
            wv_raw = raw[:, 0, :].rearrange("p (a c) -> p a c", a=WCOLS)
            nc.vector.tensor_reduce(wsum[:, :], wv_raw, AX.X, ALU.add,
                                    apply_absolute_value=True).then_inc(v_chain, 1)
            dve.wait_ge(v_chain, 1)
            nc.vector.tensor_scalar(v_down[:, :], wsum[:, :], float(np.sqrt(C)) / V_TOP, 1e-30, ALU.mult,
                                    ALU.max).then_inc(v_chain, 1)
            dve.wait_ge(v_chain, 2)
            nc.vector.reciprocal(v_up[:, :], v_down[:, :]).then_inc(v_chain, 1)
            key_sines(0, 1, 0)
            dve.wait_ge(v_chain, 3)
            for a in range(WCOLS):
                last = nc.vector.tensor_scalar(wv_raw[:, a, :], wv_raw[:, a, :], v_up[:, a:a + 1], None, ALU.mult)
            last.then_inc(v_scaled, 1)
            query_bias(0, 0)
            query_sines(0, 0, 0)
            kt_low_of(0, 0, 0, tb[0])
            query_bias(0, 1)
            query_sines(0, 1, 0)
            nc.vector.tensor_copy(bv_wide[:, :, :], bv_cols[:, :].unsqueeze(2).broadcast_to([P, WCOLS, P]))\
                .then_inc(bv_made, 1)
            kt_low_of(0, 1, 0, tb[1])
            for n in range(2):
                wv_low(n)
            qt_low_of(0, 0, tb[2])
            dve.wait_ge(ob_done, 1)
            nc.vector.tensor_tensor(out_bias[:, :], c_ps[:, 0:C], out_bias[:, :], ALU.add).then_inc(out_bias_made, 1)
            qt_low_of(0, 1, tb[0])
            for n in range(2, 4):
                wv_low(n)
            wo_raw = raw[:, 1, :].rearrange("p (a c) -> p a c", a=WCOLS)
            for a in range(WCOLS):
                last = nc.vector.tensor_scalar(wo_raw[:, a, :], wo_raw[:, a, :], v_down[:, a:a + 1], None, ALU.mult)
            last.then_inc(wo_scaled, 1)
            key_sines(1, 0, 1)

            def tops(bi, odd, g):
                dve.wait_ge(s_done, NG * bi + g + 1)
                need(p_made, NG * bi + g - 1)
                nc.vector.memset(carrier[:, 1:2], 0.0)
                for h in range(GROUP):
                    last = nc.vector.tensor_tensor_reduce(
                        out=masked[:, g % 2, h, :], in0=s_ps[:, h % 2, (h // 2) * 2 * P:(h // 2 + 1) * 2 * P],
                        in1=masks[:, 2, :] if odd else mask_even[:, :], scale=1.0, scalar=-3e38,
                        op0=ALU.add, op1=ALU.max, accum_out=top[:, g % 2, h:h + 1])
                last.then_inc(top_made, 1)
                dve.wait_ge(top_made, NG * bi + g + 1)
                nc.vector.tensor_scalar(shift[:, g % 2, :], top[:, g % 2, :], -SCALE, None,
                                        ALU.mult).then_inc(shift_made, 1)

            def ct_low_of(bi, b):
                dve.wait_ge(ct_high, 2 * bi + b + 1)
                low(ct_l[:, 4 * b:4 * b + 4, :], turn_bank("tc", b)[:, :].rearrange("p (k t) -> p k t", k=4),
                    ct_h[:, 4 * b:4 * b + 4, :], ct_low)

            dve.wait_ge(made, MADE)
            tops(0, False, 0)
            dve.wait_ge(w_high, 3)
            nc.vector.tensor_tensor(wo_l[:, :, :], wo_raw, wo_h[:, :, :].bitcast(F32),
                                    ALU.subtract).then_inc(w_low, 1)
            dve.wait_ge(w_low, 1)

            def pair(dve, j):
                for s in range(2):
                    i = 2 * j + s
                    front, ahead = exists(j, s + 1), exists(j, s + 2)

                    def context(bi, g):
                        dve.wait_ge(pv_done, NG * bi + g + 1)
                        src = c_ps[:, 0:GROUP * VE].rearrange("p (h d) -> p h d", d=VE)
                        nc.vector.reciprocal(inv[:, :, :], src[:, :, HD:VE]).then_inc(inv_made, 1)
                        dve.wait_ge(inv_made, NG * bi + g + 1)
                        nc.vector.tensor_tensor(
                            ctx[:, g * GROUP * HD:(g + 1) * GROUP * HD].rearrange("p (h d) -> p h d", d=HD),
                            src[:, :, 0:HD], inv[:, :, :].broadcast_to([P, GROUP, HD]),
                            ALU.mult).then_inc(ctx_made, 1)

                    def pt_low_of(g):
                        for half in range(2):
                            n = 2 * g + half
                            dve.wait_ge(pt_high, 2 * NG * i + n + 1)
                            low(pt_l[:, g % 2, half, :], turn_bank("pt", n)[:, :], pt_h[:, g % 2, half, :],
                                pt_low, F16)

                    tops(i, s, 1)
                    if ahead:
                        moments(i + 2, s, count(j, s + 2))
                    if front:
                        key_sines(i + 1, 1, (i + 1) % BPB)
                    if exists(j, s - 1):
                        context(i - 1, NG - 1)
                    for ch in range(2):
                        dve.wait_ge(v_high, 2 * i + ch + 1)
                        nc.vector.tensor_tensor(v_l[:, s, 8 * ch:8 * ch + 8, :],
                                                pr_ps[:, ch, :].rearrange("p (h d) -> p h d", d=HD),
                                                v_h[:, s, 8 * ch:8 * ch + 8, 0:HD], ALU.subtract).then_inc(v_low, 1)
                    pt_low_of(0)
                    tops(i, s, 2)
                    if exists(j, s - 1):
                        ct_low_of(i - 1, 0)
                    if front:
                        query_bias(i + 1, 0)
                    if ahead:
                        normalize(i + 2, s)
                    if exists(j, s - 1):
                        ct_low_of(i - 1, 1)
                    context(i, 0)
                    if front:
                        query_sines(i + 1, 0, (i + 1) % BPB)
                    tops(i, s, 3)
                    pt_low_of(1)
                    if ahead:
                        xt_low_of(i + 2, s, turn_bank("tx", 0))
                    if exists(j, s - 1):
                        dve.wait_ge(wo_done, i)
                        dve.wait_ge(res_biased, i)
                        nc.vector.tensor_tensor(x_res[:, 1 - s, :], c_ps[:, 0:C], x_res[:, 1 - s, :],
                                                ALU.add).then_inc(x_made, 1)
                    if front:
                        kt_low_of(i + 1, 0, 1 - s, turn_bank("tk", 0))
                        qt_low_of(i + 1, 0, turn_bank("tq", 0))
                        query_bias(i + 1, 1)
                        query_sines(i + 1, 1, (i + 1) % BPB)
                    context(i, 1)
                    pt_low_of(2)
                    if front:
                        if s == 1:
                            sel = ((j + 1) % (BPB // 2) + BPB // 2 - 1) // (BPB // 2)
                            nc.vector.tensor_copy(mask_even[:, :], masks[:, sel, :]).then_inc(mask_made, 1)
                            dve.wait_ge(mask_made, j + 1)
                        tops(i + 1, 1 - s, 0)
                        kt_low_of(i + 1, 1, 1 - s, turn_bank("tk", 1))
                        qt_low_of(i + 1, 1, turn_bank("tq", 1))
                    context(i, 2)
                    if ahead:
                        key_sines(i + 2, 0, (i + 2) % BPB)
                    pt_low_of(3)
            over_pairs(pair)(dve)
            dve.wait_ge(pv_done, NG * NBLK)
            src = c_ps[:, 0:GROUP * VE].rearrange("p (h d) -> p h d", d=VE)
            nc.vector.reciprocal(inv[:, :, :], src[:, :, HD:VE]).then_inc(inv_made, 1)
            dve.wait_ge(inv_made, NG * NBLK)
            nc.vector.tensor_tensor(ctx[:, 3 * GROUP * HD:QKV].rearrange("p (h d) -> p h d", d=HD),
                                    src[:, :, 0:HD], inv[:, :, :].broadcast_to([P, GROUP, HD]),
                                    ALU.mult).then_inc(ctx_made, 1)
            for b in range(2):
                ct_low_of(NBLK - 1, b)
            dve.wait_ge(wo_done, NBLK)
            dve.wait_ge(res_biased, NBLK)
            nc.vector.tensor_tensor(x_res[:, 1, :], c_ps[:, 0:C], x_res[:, 1, :], ALU.add).then_inc(x_made, 1)

        @block.scalar
        def _(act):
            def copy(out, in_, sem_):
                nc.scalar.activation(out, in_, ACT.Copy).then_inc(sem_, 1)

            def xt_high_of(t, slot, bank):
                act.wait_ge(tx_done, t + 1)
                copy(xt_h[:, slot, :, :], bank[:, 0:C].rearrange("p (k t) -> p k t", k=CK), xt_high)

            def kt_high_of(f, b, slot, bank):
                act.wait_ge(tk_done, 2 * f + b + 1)
                copy(kt_h[:, 4 * b:4 * b + 4, slot, :], bank[:, :].rearrange("p (k t) -> p k t", k=4), kt_high)

            def qt_high_of(f, b, bank):
                act.wait_ge(tq_done, 2 * f + b + 1)
                copy(qt_h[:, 4 * b:4 * b + 4, :], bank[:, :].rearrange("p (k t) -> p k t", k=4), qt_high)

            def keys_copy(f, ch):
                act.wait_ge(k_done, 2 * f + ch + 1)
                Need(act)(q_roped, 2 * (f - 1) + ch + 1)
                copy(proj[:, ch, :], pr_ps[:, ch, :], k_copied)

            def weights_high(n, col):
                act.wait_ge(raw_in[n], 16)
                copy(w_h[:, :, col:col + QKV], raw[:, n, :].rearrange("p (k c) -> p k c", k=CK), w_high)

            def wv_high(n):
                act.wait_ge(wt_done, n + 1)
                k, half = divmod(n, 2)
                copy(w_h[:, k, VC + half * 512:VC + half * 512 + 512], s_ps[:, n % 2, :], wt_high)

            weights_high(0, KC)
            xt_high_of(0, 0, tb[0])
            weights_high(1, QC)
            xt_high_of(1, 1, tb[1])
            for ch in range(2):
                keys_copy(0, ch)
            for b in range(2):
                kt_high_of(0, b, 0, tb[b])
            for n in range(2):
                wv_high(n)
            for b in range(2):
                qt_high_of(0, b, tb[(b + 2) % 3])
            for n in range(2, 4):
                wv_high(n)
            keys_copy(1, 0)
            act.wait_ge(wo_scaled, 1)
            copy(wo_h[:, :, :], raw[:, 1, :].rearrange("p (a c) -> p a c", a=WCOLS), w_high)
            keys_copy(1, 1)

            def exps(bi, g):
                act.wait_ge(shift_made, NG * bi + g + 1)
                Need(act)(pt_done, 2 * (NG * bi + g - 1))
                for h in range(GROUP):
                    last = nc.scalar.activation(prob[:, g % 2, h, :], masked[:, g % 2, h, :], ACT.Exp,
                                                bias=shift[:, g % 2, h:h + 1], scale=SCALE)
                last.then_inc(p_made, 1)

            exps(0, 0)

            def pair(act, j):
                for s in range(2):
                    i = 2 * j + s
                    front, ahead = exists(j, s + 1), exists(j, s + 2)

                    def pt_high_of(g):
                        for half in range(2):
                            n = 2 * g + half
                            act.wait_ge(pt_done, 2 * NG * i + n + 1)
                            copy(pt_h[:, g % 2, half, :], turn_bank("pt", n)[:, :], pt_high)

                    exps(i, 1)
                    for ch in range(2):
                        act.wait_ge(vp_done, 2 * i + ch + 1)
                        Need(act)(pv_done, NG * i if exists(j, s - 1) else 0)
                        copy(v_h[:, s, 8 * ch:8 * ch + 8, 0:HD],
                             pr_ps[:, ch, :].rearrange("p (h d) -> p h d", d=HD), v_high)
                    pt_high_of(0)
                    if exists(j, s - 1):
                        for b in range(2):
                            act.wait_ge(tc_done, 2 * (i - 1) + b + 1)
                            copy(ct_h[:, 4 * b:4 * b + 4, :],
                                 turn_bank("tc", b)[:, :].rearrange("p (k t) -> p k t", k=4), ct_high)
                    exps(i, 2)
                    pt_high_of(1)
                    if ahead:
                        xt_high_of(i + 2, s, turn_bank("tx", 0))
                    if front:
                        kt_high_of(i + 1, 0, 1 - s, turn_bank("tk", 0))
                        qt_high_of(i + 1, 0, turn_bank("tq", 0))
                    exps(i, 3)
                    pt_high_of(2)
                    if front:
                        kt_high_of(i + 1, 1, 1 - s, turn_bank("tk", 1))
                    if ahead:
                        keys_copy(i + 2, 0)
                    if front:
                        qt_high_of(i + 1, 1, turn_bank("tq", 1))
                        exps(i + 1, 0)
                    if ahead:
                        keys_copy(i + 2, 1)
                    pt_high_of(3)
            over_pairs(pair)(act)
            for b in range(2):
                act.wait_ge(tc_done, 2 * (NBLK - 1) + b + 1)
                copy(ct_h[:, 4 * b:4 * b + 4, :], turn_bank("tc", b)[:, :].rearrange("p (k t) -> p k t", k=4),
                     ct_high)

        @block.tensor
        def _(pe):
            need = Need(pe)
            w = (w_h, w_l)
            wo = (wo_h, wo_l)
            xt = (xt_h, xt_l)

            def transpose_x(t, bank):
                pe.wait_ge(xn_made, t + 1)
                for k in range(CK):
                    last = nc.tensor.transpose(bank[:, k * P:(k + 1) * P], xn[:, k * P:(k + 1) * P], ident[:, :])
                last.then_inc(tx_done, 1)

            def project(slot, ch, col, done):
                for n, (xp, wp) in enumerate(TERMS):
                    for k in range(CK):
                        last = nc.tensor.matmul(pr_ps[:, ch, :], xt[xp][:, slot, k, :], w[wp][:, k, col:col + 512],
                                                start=n == 0 and k == 0,
                                                stop=n == 2 and k == CK - 1)
                last.then_inc(done, 1)

            def key(f, ch, slot):
                need(q_biased, 2 * (f - 1) + ch + 1)
                project(slot, ch, KC + ch * 512, k_done)

            def query(ch, slot, read, read_count):
                pe.wait_ge(read, read_count + ch + 1)
                project(slot, ch, QC + ch * 512, q_done)

            def transpose_context(b, bank):
                for a in range(4):
                    last = nc.tensor.transpose(bank[:, a * P:(a + 1) * P],
                                               ctx[:, (4 * b + a) * P:(4 * b + a + 1) * P], ident[:, :])
                last.then_inc(tc_done, 1)

            def transpose_rope(f, b, src, roped, bank, done):
                pe.wait_ge(roped, 2 * f + b + 1)
                for a in range(4):
                    last = nc.tensor.transpose(bank[:, a * P:(a + 1) * P], src[:, b, a * P:(a + 1) * P], ident[:, :])
                last.then_inc(done, 1)

            def output(bi):
                pe.wait_ge(ct_low, 2 * (bi + 1))
                if isinstance(bi, int) and bi == 0:
                    pe.wait_ge(w_low, 1)
                    pe.wait_ge(out_bias_made, 1)
                for n, (xp, wp) in enumerate(TERMS):
                    for a in range(WCOLS):
                        last = nc.tensor.matmul(c_ps[:, 0:C], (ct_h, ct_l)[xp][:, a, :], wo[wp][:, a, :],
                                                start=n == 0 and a == 0, stop=n == 2 and a == WCOLS - 1)
                last.then_inc(wo_done, 1)

            def values_product(g):
                for h in range(GROUP):
                    head = g * GROUP + h
                    out = c_ps[:, h * VE:h * VE + VE]
                    for slot in range(2):
                        ph = pt_h[:, g % 2, h // 2, ((h % 2) * 2 + slot) * P:((h % 2) * 2 + slot + 1) * P]
                        pl = pt_l[:, g % 2, h // 2, ((h % 2) * 2 + slot) * P:((h % 2) * 2 + slot + 1) * P]
                        nc.tensor.matmul(out, ph, v_h[:, slot, head, :], start=slot == 0, stop=False)
                        nc.tensor.matmul(out[:, 0:HD], ph, v_l[:, slot, head, :], start=False, stop=False)
                        last = nc.tensor.matmul(out, pl, v_h[:, slot, head, :], start=False, stop=slot == 1)
                last.then_inc(pv_done, 1)

            pe.wait_ge(made, 3)
            for t in range(AHEAD):
                transpose_x(t, tb[t])
            def wv_transposes(n):
                pe.wait_ge(v_scaled, 1)
                k, half = divmod(n, 2)
                need(wt_low, n - 1)
                for a in range(4):
                    o = 4 * half + a
                    last = nc.tensor.transpose(s_ps[:, n % 2, a * P:(a + 1) * P],
                                               raw[:, 0, o * C + k * P:o * C + (k + 1) * P], ident[:, :])
                last.then_inc(wt_done, 1)

            pe.wait_ge(xt_low, 1)
            pe.wait_ge(w_free, 1)
            for ch in range(2):
                key(0, ch, 0)
            pe.wait_ge(w_free, 2)
            for ch in range(2):
                query(ch, 0, k_copied, 0)
            pe.wait_ge(xt_low, AHEAD)
            for b in range(2):
                transpose_rope(0, b, k_rope, k_roped, tb[b], tk_done)
            for n in range(2):
                wv_transposes(n)
            transpose_rope(0, 0, q_rope, q_roped, tb[2], tq_done)
            pe.wait_ge(bv_made, 1)
            pe.wait_ge(raw_in[1], 32)
            for a in range(WCOLS):
                last = nc.tensor.matmul(c_ps[:, 0:C], bv_wide[:, a, :],
                                        raw[:, 1, a * C:(a + 1) * C], start=a == 0, stop=a == WCOLS - 1)
            last.then_inc(ob_done, 1)
            pe.wait_ge(kt_low, 1)
            transpose_rope(0, 1, q_rope, q_roped, tb[0], tq_done)
            for n in range(2, 4):
                wv_transposes(n)
            for ch in range(2):
                key(1, ch, 1)
            pe.wait_ge(wt_low, 4)

            def scores(bi, g):
                pe.wait_ge(qt_low, 2 * bi + g // 2 + 1)
                pe.wait_ge(kt_low, 2 * bi + g // 2 + 1)
                need(top_made, NG * bi + g)
                for a in range(2):
                    for n, (qp, kp) in enumerate(TERMS):
                        for e in range(2):
                            rows = slice(e * HD, (e + 1) * HD)
                            last = nc.tensor.matmul(
                                s_ps[:, e, a * 2 * P:(a + 1) * 2 * P],
                                (qt_h, qt_l)[qp][rows, 2 * g + a, :],
                                (kt_h, kt_l)[kp][rows, 2 * g + a, :, :].rearrange("p s t -> p (s t)"),
                                start=n == 0, stop=n == 2)
                last.then_inc(s_done, 1)

            scores(0, 0)

            def pair(pe, j):
                for s in range(2):
                    i = 2 * j + s
                    front, ahead = exists(j, s + 1), exists(j, s + 2)

                    def transpose_prob(g):
                        pe.wait_ge(p_made, NG * i + g + 1)
                        for half in range(2):
                            wait_turn(pe, "pt", 2 * g + half, i)
                            bank = turn_bank("pt", 2 * g + half)
                            for a in range(4):
                                h, slot = 2 * half + a // 2, a % 2
                                last = nc.tensor.transpose(bank[:, a * P:(a + 1) * P],
                                                           prob[:, g % 2, h, slot * P:(slot + 1) * P], ident[:, :])
                            last.then_inc(pt_done, 1)

                    scores(i, 1)
                    for ch in range(2):
                        if front:
                            pe.wait_ge(k_copied, 2 * (i + 1) + ch + 1)
                        else:
                            pe.wait_ge(q_biased, 2 * i + ch + 1)
                        project(s, ch, VC + ch * 512, vp_done)
                    if exists(j, s - 1):
                        pe.wait_ge(pt_low, 2 * NG * i)
                        pe.wait_ge(ctx_made, NG * i - 1)
                        values_product(NG - 1)
                    transpose_prob(0)
                    scores(i, 2)
                    if exists(j, s - 1):
                        pe.wait_ge(ctx_made, NG * i)
                    for b in range(2):
                        if exists(j, s - 1):
                            wait_turn(pe, "tc", b, i)
                            transpose_context(b, turn_bank("tc", b))
                        if front:
                            query(b, 1 - s, v_low, 2 * i)
                    pe.wait_ge(v_low, 2 * i + 2)
                    pe.wait_ge(pt_low, 2 * NG * i + 2)
                    values_product(0)
                    transpose_prob(1)
                    scores(i, 3)
                    if ahead:
                        wait_turn(pe, "tx", 0, i)
                        transpose_x(i + 2, turn_bank("tx", 0))
                    pe.wait_ge(ctx_made, NG * i + 1)
                    if exists(j, s - 1):
                        output(i - 1)
                    if front:
                        wait_turn(pe, "tk", 0, i)
                        transpose_rope(i + 1, 0, k_rope, k_roped, turn_bank("tk", 0), tk_done)
                        wait_turn(pe, "tq", 0, i)
                        transpose_rope(i + 1, 0, q_rope, q_roped, turn_bank("tq", 0), tq_done)
                    pe.wait_ge(pt_low, 2 * NG * i + 4)
                    if exists(j, s - 1):
                        pe.wait_ge(x_made, i)
                    values_product(1)
                    transpose_prob(2)
                    if front:
                        scores(i + 1, 0)
                        wait_turn(pe, "tk", 1, i)
                        transpose_rope(i + 1, 1, k_rope, k_roped, turn_bank("tk", 1), tk_done)
                    for ch in range(2):
                        if front and ch == 1:
                            wait_turn(pe, "tq", 1, i)
                            transpose_rope(i + 1, 1, q_rope, q_roped, turn_bank("tq", 1), tq_done)
                        if ahead:
                            pe.wait_ge(xt_low, i + 3)
                            key(i + 2, ch, s)
                    pe.wait_ge(pt_low, 2 * NG * i + 6)
                    pe.wait_ge(ctx_made, NG * i + 2)
                    values_product(2)
                    transpose_prob(3)
            over_pairs(pair)(pe)
            pe.wait_ge(pt_low, 2 * NG * NBLK)
            pe.wait_ge(ctx_made, NG * NBLK - 1)
            values_product(NG - 1)
            pe.wait_ge(ctx_made, NG * NBLK)
            for b in range(2):
                wait_turn(pe, "tc", b, NBLK)
                transpose_context(b, turn_bank("tc", b))
            output(NBLK - 1)


def build(nc, x, wa_t, ba, wq_t, bq, wk_t, bk, wv, bv, wo_t, bo, wr_t, wkk_t, wvv_t, mu_r, mu_k, cos, sin, sin_neg,
          out):
    x1 = nc.dram_tensor("x_after_ffn", (P, NBLK, C), F32, kind="Internal").ap()
    x2 = nc.dram_tensor("x_after_attention", (P, NBLK, C), F32, kind="Internal").ap()
    with ExitStack() as sems:
        tiles = ffn_constants(nc, sems)
        ffn_phase(nc, sems, "f1", x, x1, tiles, weights=(wr_t, wkk_t, wvv_t, mu_r, mu_k), value=(wa_t, ba))
        attention_phase(nc, sems, x1, x2, wq_t, wk_t, wv, wo_t, bq, bk, bv, bo, cos, sin, sin_neg)
        ffn_phase(nc, sems, "f2", x2, out, tiles)


def rope_tables():
    freq = (1.0 / np.power(np.float32(10000.0), np.arange(0, HD, 2, dtype=np.float32) / np.float32(HD))).astype(np.float32)
    angle = np.arange(SEQ, dtype=np.float32)[:, None] * freq[None, :]
    lay = lambda a: np.ascontiguousarray(a.astype(np.float32).reshape(BPB, P, HD // 2).transpose(1, 0, 2))
    return lay(np.cos(angle)), lay(np.sin(angle)), lay(-np.sin(angle))


def kernel(**inputs):
    import numpy as _np
    import concourse.bacc as _bacc
    from concourse import mybir as _mybir
    from concourse.bass_utils import run_bass_kernel_spmd as _run

    lay = _np.ascontiguousarray
    a = {name: _np.asarray(value) for name, value in inputs.items()}
    cos, sin, sin_neg = rope_tables()
    arrays = {
        "x": lay(a["L0_attn_a_x"].reshape(NBLK, P, C).transpose(1, 0, 2)),
        "wa_t": lay(a["L0_attn_a_W"].T), "ba": lay(a["L0_attn_a_b"]),
        "wq_t": lay(a["L0_attn_b_Wq"].T), "bq": lay(a["L0_attn_b_bq"]),
        "wk_t": lay(a["L0_attn_b_Wk"].T), "bk": lay(a["L0_attn_b_bk"]),
        "wv": lay(a["L0_attn_b_Wv"]), "bv": lay(a["L0_attn_b_bv"].reshape(QKV // P, P).T),
        "wo_t": lay(a["L0_attn_b_Wo"].T), "bo": lay(a["L0_attn_b_bo"]),
        "wr_t": lay(a["L0_ffn_W_r"].T), "wkk_t": lay(a["L0_ffn_W_k"].T), "wvv_t": lay(a["L0_ffn_W_v"].T),
        "mu_r": lay(a["L0_ffn_mu_r"].reshape(CK, P).T), "mu_k": lay(a["L0_ffn_mu_k"].reshape(CK, P).T),
        "cos": cos, "sin": sin, "sin_neg": sin_neg,
    }
    nc = _bacc.Bacc("TRN2", target_bir_lowering=False, num_devices=1)
    args = [nc.dram_tensor(f"in_{n}", v.shape, _mybir.dt.from_np(v.dtype), kind="ExternalInput").ap()
            for n, v in arrays.items()]
    out = nc.dram_tensor("out_x", (P, NBLK, C), _mybir.dt.float32, kind="ExternalOutput").ap()
    build(nc, *args, out)
    r = _run(nc, [{f"in_{n}": v for n, v in arrays.items()}], core_ids=[0])
    got = r.results[0]["out_x"]
    return lay(got.transpose(1, 0, 2)).reshape(BATCH, SEQ, C)
```
